# Optimizing a Trainium2 kernel written in Bass

```python
import numpy as np
import jax
import jax.numpy as jnp

def _softmax(x, axis=-1):
    return jax.nn.softmax(x, axis=axis)

def _gelu(x):
    return jax.nn.gelu(x, approximate=True)

def _silu(x):
    return jax.nn.silu(x)

def _sigmoid(x):
    return jax.nn.sigmoid(x)

def _layernorm(x, axis=-1, eps=1e-05):
    m = jnp.mean(x, axis=axis, keepdims=True)
    v = jnp.var(x, axis=axis, keepdims=True)
    return (x - m) / jnp.sqrt(v + eps)

def _scatter_add(tgt, idx, src, axis=0):
    return tgt.at[idx].add(src)

def _segment_sum(src, seg, n):
    return jax.ops.segment_sum(src, seg, n)
kernel_name = 'mk_seq_preln_d1_jaxref_r8_ee496f'

def setup_inputs(seed: int=0):
    np.random.seed(seed)
    _w = jnp.asarray

    def _L0_attn_setup():
        import jax, jax.numpy as jnp
        import numpy as np
        N_EMBED = 256
        N_HEAD = 16
        N_KV_HEAD = 4
        HEAD_DIM = N_EMBED // N_HEAD
        REPEAT = N_HEAD // N_KV_HEAD
        THETA = 10000.0

        def _rope_angles(T):
            freqs = THETA ** (-(jnp.arange(0, N_EMBED, 2, dtype=jnp.float32) / N_EMBED))
            freqs = freqs[:HEAD_DIM // 2]
            t = jnp.arange(T, dtype=jnp.float32)
            return jnp.outer(t, freqs)

        def _apply_rope(x, cos, sin):
            xr = x[..., 0::2]
            xi = x[..., 1::2]
            or_ = xr * cos - xi * sin
            oi_ = xr * sin + xi * cos
            out = jnp.stack([or_, oi_], axis=-1).reshape(x.shape)
            return out.astype(jnp.bfloat16).astype(jnp.float32)
        key = jax.random.key(seed)
        ks = jax.random.split(key, 9)
        B, T = (2, 256)
        s = 0.02
        return {'x': jax.random.normal(ks[0], (B, T, N_EMBED), jnp.float32), 'Wq': jax.random.normal(ks[1], (N_EMBED, N_EMBED), jnp.float32) * s, 'bq': jax.random.normal(ks[2], (N_EMBED,), jnp.float32) * s, 'Wk': jax.random.normal(ks[3], (N_EMBED, N_KV_HEAD * HEAD_DIM), jnp.float32) * s, 'bk': jax.random.normal(ks[4], (N_KV_HEAD * HEAD_DIM,), jnp.float32) * s, 'Wv': jax.random.normal(ks[5], (N_EMBED, N_KV_HEAD * HEAD_DIM), jnp.float32) * s, 'bv': jax.random.normal(ks[6], (N_KV_HEAD * HEAD_DIM,), jnp.float32) * s, 'Wo': jax.random.normal(ks[7], (N_EMBED, N_EMBED), jnp.float32) * s, 'bo': jax.random.normal(ks[8], (N_EMBED,), jnp.float32) * s}
    _L0_attn_in = _L0_attn_setup()

    def _L0_ffn_setup():
        import jax, jax.numpy as jnp
        import numpy as np
        B, S, H = (2, 64, 256)
        E, I, K = (64, 176, 6)
        NS = 2
        SH_I = I * NS
        key = jax.random.key(seed)
        ks = jax.random.split(key, 6)
        s = 0.02
        return {'hidden_states': jax.random.normal(ks[0], (B, S, H), jnp.float32), 'gate_w': jax.random.normal(ks[1], (E, H), jnp.float32) * s, 'experts_w1': jax.random.normal(ks[2], (E, I, H), jnp.float32) * s, 'experts_w2': jax.random.normal(ks[3], (E, H, I), jnp.float32) * s, 'shared_gate_up': jax.random.normal(ks[4], (2 * SH_I, H), jnp.float32) * s, 'shared_down': jax.random.normal(ks[5], (H, SH_I), jnp.float32) * s}
    _L0_ffn_in = _L0_ffn_setup()
    _d = {'L0_attn_x': _L0_attn_in['x'], 'L0_attn_Wq': _L0_attn_in['Wq'], 'L0_attn_bq': _L0_attn_in['bq'], 'L0_attn_Wk': _L0_attn_in['Wk'], 'L0_attn_bk': _L0_attn_in['bk'], 'L0_attn_Wv': _L0_attn_in['Wv'], 'L0_attn_bv': _L0_attn_in['bv'], 'L0_attn_Wo': _L0_attn_in['Wo'], 'L0_attn_bo': _L0_attn_in['bo'], 'L0_ffn_gate_w': _L0_ffn_in['gate_w'], 'L0_ffn_experts_w1': _L0_ffn_in['experts_w1'], 'L0_ffn_experts_w2': _L0_ffn_in['experts_w2'], 'L0_ffn_shared_gate_up': _L0_ffn_in['shared_gate_up'], 'L0_ffn_shared_down': _L0_ffn_in['shared_down']}
    _x0 = _d['L0_attn_x']
    _d['L0_attn_x'] = jax.random.normal(jax.random.fold_in(jax.random.key(seed), 1), (1, 2048, 256), dtype=_x0.dtype)
    del _x0
    return _d

def reference(L0_attn_x, L0_attn_Wq, L0_attn_bq, L0_attn_Wk, L0_attn_bk, L0_attn_Wv, L0_attn_bv, L0_attn_Wo, L0_attn_bo, L0_ffn_gate_w, L0_ffn_experts_w1, L0_ffn_experts_w2, L0_ffn_shared_gate_up, L0_ffn_shared_down):

    def _L0_attn_ref(x, Wq, bq, Wk, bk, Wv, bv, Wo, bo):
        import jax, jax.numpy as jnp
        import numpy as np
        N_EMBED = 256
        N_HEAD = 16
        N_KV_HEAD = 4
        HEAD_DIM = N_EMBED // N_HEAD
        REPEAT = N_HEAD // N_KV_HEAD
        THETA = 10000.0

        def _rope_angles(T):
            freqs = THETA ** (-(jnp.arange(0, N_EMBED, 2, dtype=jnp.float32) / N_EMBED))
            freqs = freqs[:HEAD_DIM // 2]
            t = jnp.arange(T, dtype=jnp.float32)
            return jnp.outer(t, freqs)

        def _apply_rope(x, cos, sin):
            xr = x[..., 0::2]
            xi = x[..., 1::2]
            or_ = xr * cos - xi * sin
            oi_ = xr * sin + xi * cos
            out = jnp.stack([or_, oi_], axis=-1).reshape(x.shape)
            return out.astype(jnp.bfloat16).astype(jnp.float32)
        B, T, _ = x.shape
        q = (x @ Wq + bq).reshape(B, T, N_HEAD, HEAD_DIM)
        k = (x @ Wk + bk).reshape(B, T, N_KV_HEAD, HEAD_DIM)
        v = (x @ Wv + bv).reshape(B, T, N_KV_HEAD, HEAD_DIM)
        ang = _rope_angles(T)
        cos = jnp.cos(ang)[None, :, None, :]
        sin = jnp.sin(ang)[None, :, None, :]
        xq = _apply_rope(q, cos, sin)
        xk = _apply_rope(k, cos, sin)
        xq = xq.transpose(0, 2, 1, 3)
        xk = xk.transpose(0, 2, 1, 3)
        xv = v.transpose(0, 2, 1, 3)
        xk = jnp.repeat(xk, REPEAT, axis=1)
        xv = jnp.repeat(xv, REPEAT, axis=1)
        qk = jnp.einsum('bhtd,bhsd->bhts', xq, xk)
        causal = jnp.tril(jnp.ones((T, T), dtype=bool))
        qk = jnp.where(causal[None, None], qk, -jnp.inf)
        attn = jax.nn.softmax(qk, axis=-1) * N_EMBED ** (-0.5)
        o = jnp.einsum('bhts,bhsd->bhtd', attn, xv)
        o = o.transpose(0, 2, 1, 3).reshape(B, T, N_EMBED)
        return o @ Wo + bo

    def _L0_ffn_ref(hidden_states, gate_w, experts_w1, experts_w2, shared_gate_up, shared_down):
        import jax, jax.numpy as jnp
        import numpy as np
        B, S, H = (2, 64, 256)
        E, I, K = (64, 176, 6)
        NS = 2
        SH_I = I * NS
        orig_shape = hidden_states.shape
        x = hidden_states.reshape(-1, orig_shape[-1])
        router_logits = x @ gate_w.T
        probs = jax.nn.softmax(router_logits, axis=-1)
        topk_w, topk_idx = jax.lax.top_k(probs, K)
        topk_w = topk_w / jnp.sum(topk_w, axis=-1, keepdims=True)
        combine = jnp.sum(jax.nn.one_hot(topk_idx, E, dtype=x.dtype) * topk_w[..., None], axis=1)
        h = jax.nn.silu(jnp.einsum('th,eih->tei', x, experts_w1))
        y = jnp.einsum('tei,ehi->teh', h, experts_w2)
        routed_out = jnp.einsum('teh,te->th', y, combine)
        gu = x @ shared_gate_up.T
        g, u = jnp.split(gu, 2, axis=-1)
        shared_out = jax.nn.silu(g) * u @ shared_down.T
        return (routed_out + shared_out).reshape(orig_shape)
    x = L0_attn_x
    x = x + _L0_attn_ref(_layernorm(x, axis=-1), L0_attn_Wq, L0_attn_bq, L0_attn_Wk, L0_attn_bk, L0_attn_Wv, L0_attn_bv, L0_attn_Wo, L0_attn_bo)
    x = x + _L0_ffn_ref(_layernorm(x, axis=-1), L0_ffn_gate_w, L0_ffn_experts_w1, L0_ffn_experts_w2, L0_ffn_shared_gate_up, L0_ffn_shared_down)
    return x

_drawn_inputs = setup_inputs


def setup_inputs(seed=0):
    import zlib

    import numpy as np

    out = dict(_drawn_inputs(seed))
    spreads = {}
    factors = {'L0_attn_Wq': 8.0,
     'L0_attn_bq': 8.0,
     'L0_attn_Wk': 8.0,
     'L0_attn_bk': 8.0,
     'L0_attn_Wv': 8.0,
     'L0_attn_bv': 8.0,
     'L0_attn_Wo': 8.0,
     'L0_attn_bo': 2.923,
     'L0_ffn_gate_w': 3.168,
     'L0_ffn_experts_w1': 2.965,
     'L0_ffn_experts_w2': 2.952,
     'L0_ffn_shared_gate_up': 2.832,
     'L0_ffn_shared_down': 2.832}
    for name, (base, spread) in spreads.items():
        noise = np.random.default_rng([zlib.crc32(name.encode()), seed]).standard_normal(out[name].shape)
        drawn = base * np.exp(spread * noise) if base else spread * noise
        out[name] = jnp.asarray(drawn.astype(out[name].dtype))
    for name, factor in factors.items():
        out[name] = (out[name] * factor).astype(out[name].dtype)
    return out
```

```python
import concourse.bass as bass
from concourse import mybir
from contextlib import ExitStack
import numpy as np

T, H = 2048, 256
NH, NKV, HD = 16, 4, 16
E, I, K = 64, 176, 6
SI = 2 * I
P = 128
NT = T // P
QB = 512
NB = T // QB
J = NH // NKV
HI = I // 2
CH = H // P
UNITS = NB * NKV
MROWS = 3
NBLK = 160
DUMP = T * K
EPS = 1e-5
BIG = -1.0e30


def preln_attention_moe(nc, x, w_qkv, b_q, b_k, b_v, b_o, w_o, gate, w_sh1, w_sh2, w1, w2, trig, cst, out):
    f32, bf16, i32, u32 = mybir.dt.float32, mybir.dt.bfloat16, mybir.dt.int32, mybir.dt.uint32
    ALU, ACT, AX = mybir.AluOpType, mybir.ActivationFunctionType, mybir.AxisListType
    ds = bass.ds

    xn2_d = nc.dram_tensor("xn2_rows", [T, H], f32).ap()
    table_d = nc.dram_tensor("slot_table", [P * NBLK, 2], i32).ap()
    y_d = nc.dram_tensor("expert_rows", [DUMP + NBLK * P, H], f32).ap()

    ctx = ExitStack()
    with ctx:
        def sb(name, shape, dt=f32):
            return ctx.enter_context(nc.sbuf_tensor(name, shape, dt))

        def sem(name):
            return ctx.enter_context(nc.semaphore(name))

        x_sb = sb("x_sb", [P, NT * H])
        wqkv = sb("wqkv", [P, CH, 384])
        bq, bk = sb("bq", [P, 2]), sb("bk", [32, 2])
        bv, bo = sb("bv", [P, NKV * HD]), sb("bo", [P, H])
        wo = sb("wo", [P, NKV, H])
        gate_sb = sb("gate_sb", [P, CH, E])
        sh1 = sb("sh1", [P, CH, 2 * SI])
        sh2 = sb("sh2", [HI, 4, H])
        c_sb = sb("c_sb", [P, cst.shape[1]])
        ident = c_sb[:, 0:128]
        qmask = c_sb[:, 128:640]
        kmask = c_sb[:, 640:768]
        iota_e = c_sb[:, 768:832]
        tri_before = c_sb[0:E, 832:896]
        tri_upto = c_sb[0:E, 896:960]
        blk_start = c_sb[0:E, 960:960 + NBLK]
        ones_col = c_sb[0:E, 1120:1121]
        ident16 = sb("ident16", [P, P], bf16)
        kmask16 = sb("kmask16", [P, P], bf16)
        stats = sb("stats", [P, NT, 6])
        mv = sb("mv", [P, NT * 2])
        rstd = sb("rstd", [P, NT])
        rs_tmp = sb("rs_tmp", [P, 2, NT])
        xn = sb("xn", [P, 4, H])
        xnT = sb("xnT", [P, CH, QB])
        q_aug = sb("q_aug", [P, UNITS, QB], bf16)
        k_pad = sb("k_pad", [P, J, NKV * T], bf16)
        v_all = sb("v_all", [P, NKV * NT * 32])
        v_cur = sb("v_cur", [P, NT, 32])
        p_ring = sb("p_ring", [P, 8, QB])
        o_nrm = sb("o_nrm", [P, UNITS * QB])
        cos, sin = o_nrm[:, 0:T], o_nrm[:, T:2 * T]
        rot = o_nrm[:, 2 * T:4 * T].bitcast(bf16).rearrange("p (a t) -> p a t", a=4)
        xn2T = sb("xn2T", [P, CH, T])
        m_part = sb("m_part", [P, 16, NB])
        m_row, m_neg, m_r1, m_r2 = sb("m_row", [P, 16]), sb("m_neg", [P, 16]), sb("m_r1", [P, 16]), sb("m_r2", [P, 16])
        m_stage = sb("m_stage", [P, 4, P], bf16)
        m_T = sb("m_T", [P, QB], bf16)
        xn_flat = xn[:, :, :].rearrange("p n h -> p (n h)")
        scale = xn_flat[:, 0:QB]
        heads, scale_row = xnT[:, 0, :], xnT[:, 1, :]
        sums, inv_sums = sb("sums", [P, 16]), sb("inv_sums", [P, 16])
        places = {"k_pad": [k_pad[:, :, :].rearrange("p a b -> p (a b)").bitcast(f32), 0, J * NKV * T // 2],
                  "o_nrm": [o_nrm[:, :], 0, UNITS * QB],
                  "p_ring": [p_ring[:, :, :].rearrange("p a b -> p (a b)"), 0, 8 * QB],
                  "q_aug": [q_aug[:, :, :].rearrange("p a b -> p (a b)").bitcast(f32), 0, UNITS * QB // 2]}

        def lt(n, dt=f32, rows=P, where="k_pad"):
            ap, at, size = places[where]
            places[where][1] += n
            assert at + n <= size, where
            return ap[0:rows, at:at + n] if dt == f32 else ap[0:rows, at:at + n].bitcast(dt)

        o_cur = lt(NKV * QB).rearrange("p (g t) -> p g t", g=NKV)
        hot = lt(NT * K * E // 2, bf16)
        chosen = lt(NT * E // 2, bf16)
        cum, hotT, ones_row = lt(T, rows=E), lt(T, rows=E), lt(T, rows=E)
        prod = lt(NT * K * E // 2, where="o_nrm")
        lg, ex, pr = lt(4 * E), lt(4 * E), lt(4 * E)
        row4, sum4, sum6 = lt(4), lt(4), lt(4)
        top8, idx8, idxf = lt(32), lt(32, u32), lt(32)
        wts = lt(NT * K)
        slot, slot_i, smod, sdiv, srow = (lt(NT * K, t) for t in (f32, i32, i32, i32, i32))
        src2 = lt(NT * K * 2, i32)
        tab0, tab = lt(NBLK * 2, i32), lt(NBLK * 2, i32)
        cnt = lt(8, rows=E)
        past_end = lt(NBLK, rows=E)
        eob = lt(NBLK, i32, rows=1)
        sg = lt(2 * QB, rows=HI).rearrange("p (a t) -> p a t", a=2)
        hs = o_cur[0:HI, :, :]
        w1s = [lt(CH * I, where="q_aug").rearrange("p (c i) -> p c i", c=CH) for _ in range(4)]
        w2s = [lt(2 * H, rows=HI, where="q_aug").rearrange("p (c n) -> p c n", c=2) for _ in range(4)]
        ids_x, ids_y = [lt(1, i32) for _ in range(4)], [lt(1, i32) for _ in range(4)]
        xg, ys = [lt(H, where="o_nrm") for _ in range(4)], [lt(H, where="o_nrm") for _ in range(4)]
        xgT = [lt(H, where="o_nrm") for _ in range(2)]
        hT = [lt(2 * P, rows=HI, where="o_nrm") for _ in range(2)]
        yk = [lt(K * H, where="p_ring") for _ in range(2)]
        acc = [lt(H, where="p_ring") for _ in range(2)]

        bank = [ctx.enter_context(nc.psum_tensor(f"bank{n}", [P, 512], f32)) for n in range(8)]
        bank16 = [b[:, :].bitcast(bf16) for b in bank]
        S_Q = bank[0:4]
        S_K = bank[4:6]
        PV = bank[6]

        passed = sem("passed")
        ld_x = [sem(f"ld_x{n}") for n in range(4)]
        (ld_w, ld_c, ld_late, consts16, q_zeroed, k_zeroed, v_ones, dve, pool) = map(sem, (
            "ld_w", "ld_c", "ld_late", "consts16", "q_zeroed", "k_zeroed", "v_ones", "dve_chain", "pool_chain"))
        (xn_ready, xn_used, xnT_ready, q_mm, k_mm, v_mm, rot_terms, rot_done, qk_placed, v_done) = map(sem, (
            "xn_ready", "xn_used", "xnT_ready", "q_mm", "k_mm", "v_mm", "rot_terms", "rot_done",
            "qk_placed", "v_done"))
        (sq_ready, sq_used, sk_ready, p_ready, pv_done, v_staged, max_ready, split_done, mT_ready, mT_copied,
         mrow_placed, o_done, pv_copied, sums_moved, inverted, inv_moved, scale_ready,
         scale_row_set, xb_done) = map(sem, (
            "sq_ready", "sq_used", "sk_ready", "p_ready", "pv_done", "v_staged", "max_ready", "split_done",
            "mT_ready", "mT_copied", "mrow_placed", "o_done", "pv_copied", "sums_moved", "inverted",
            "inv_moved", "scale_ready", "scale_row_set", "xb_done"))
        (o_loaded, wo_mm, x1_done, xn2_ready, xn2_used, xn2_stored, xn2T_ready, xn2T_all, logit_mm, logit_sub,
         exp_done, chosen_ready) = map(sem, (
            "o_loaded", "wo_mm", "x1_done", "xn2_ready", "xn2_used", "xn2_stored", "xn2T_ready", "xn2T_all",
            "logit_mm", "logit_sub", "exp_done", "chosen_ready"))
        (hot_mm, hotT_done, late_consts, table_init, padded, base_mm, slotT_ready, slotT_mm, past_ready, eob_mm,
         eob_ready, srow_ready, scattered, tab_loaded) = map(sem, (
            "hot_mm", "hotT_done", "late_consts", "table_init", "padded", "base_mm", "slotT_ready", "slotT_mm",
            "past_ready", "eob_mm", "eob_ready", "srow_ready", "scattered", "tab_loaded"))
        (sh_mm, sg_ready, hs_ready, shd_mm, sh_added) = map(sem, (
            "sh_mm", "sg_ready", "hs_ready", "shd_mm", "sh_added"))
        w_loaded = [sem(f"w_loaded{n}") for n in range(4)]
        xg_loaded = [sem(f"xg_loaded{n}") for n in range(4)]
        y_stored = [sem(f"y_stored{n}") for n in range(4)]
        (idx_ready, idy_ready, xg_T, xgT_ready, up_mm, h_ready, down_mm, y_ready, summed) = map(sem, (
            "idx_ready", "idy_ready", "xg_T", "xgT_ready", "up_mm", "h_ready", "down_mm", "y_ready", "summed"))
        yk_loaded = [sem(f"yk_loaded{n}") for n in range(2)]
        out_stored = [sem(f"out_stored{n}") for n in range(2)]

        def wait(eng, s, value):
            if not isinstance(value, int) or value > 0:
                eng.wait_ge(s, value)

        def wait_apart(eng, s, value):
            wait(eng, s, value)
            if not isinstance(value, int):
                eng.sem_inc(passed, 1)

        class Chain:

            def __init__(self, eng, s):
                self.eng, self.s, self.base, self.n = eng, s, 0, 0

            def link(self, ins):
                self.n += 1
                ins.then_inc(self.s, 1)
                wait_apart(self.eng, self.s, self.base + self.n)

            def enter(self, step, per):
                self.start, self.per = self.base + self.n, per
                self.base, self.n = step * per + self.start, 0

            def leave(self, steps):
                assert self.n == self.per
                self.base, self.n = self.start + steps * self.per, 0

        def key_tiles(b):
            return 4 * (b + 1)

        def tiles_before(b, g):
            return g * key_tiles(b) + 8 * b * (b + 1)

        def maxes_before(b, g):
            return g * (16 * (b + 1)) + 32 * b * (b + 1)

        def max_chunks(b):
            return [(tt, c, j) for tt in range(4) for c in range(b + 1) for j in range(J)]

        def bodies(eng, body):
            for g in range(2):
                body(0, g, 0, g + 2)
            for b in range(NB):
                if b:
                    with eng.Fori(0, 2) as g:
                        body(b, g, b, g + 2)
                if b + 1 < NB:
                    with eng.Fori(0, 2) as g:
                        body(b, g + 2, b + 1, g)
            for g in range(2):
                body(NB - 1, g + 2, None, g)

        def has_next(mb, mg):
            return mb is not None or mg == 0

        block = ctx.enter_context(nc.Block())

        @block.sync
        def _(sp):
            xt = x.rearrange("o (n p) h -> p (o n) h", p=P)
            xv = x_sb[:, :].rearrange("p (n h) -> p n h", h=H)
            sp.dma_start(xv[:, 0:4, :], xt[:, 0:4, :]).then_inc(ld_x[0], 16)
            sp.dma_start(c_sb[:, :], cst).then_inc(ld_c, 16)
            for n in range(1, 4):
                sp.dma_start(xv[:, 4 * n:4 * n + 4, :], xt[:, 4 * n:4 * n + 4, :]).then_inc(ld_x[n], 16)
            sp.dma_start(wqkv[:, :, :], w_qkv).then_inc(ld_w, 16)
            sp.dma_start(bq[:, :], b_q).then_inc(ld_w, 16)
            sp.dma_start(bk[:, :], b_k).then_inc(ld_w, 16)
            sp.dma_start(bv[:, :], b_v).then_inc(ld_w, 16)
            sp.dma_start(bo[:, :], b_o).then_inc(ld_w, 16)
            sp.dma_start(o_nrm[:, 0:2 * T], trig).then_inc(ld_w, 16)
            sp.dma_start(wo[:, :, :], w_o).then_inc(ld_late, 16)
            sp.dma_start(gate_sb[:, :, :], gate).then_inc(ld_late, 16)
            sp.dma_start(sh1[:, :, :], w_sh1).then_inc(ld_late, 16)
            sp.dma_start(sh2[:, :, :], w_sh2).then_inc(ld_late, 16)
            sp.wait_ge(q_zeroed, 1)
            sp.wait_ge(k_zeroed, 1)
            sp.wait_ge(rot_done, 4 * NB + 4)
            q_rows = q_aug[:, :, :].rearrange("p (b g) t -> p b g t", b=NB)
            for g in range(NKV):
                for j in range(J):
                    for part in range(2):
                        row = 32 * j + MROWS + 8 * part
                        src = 32 * j + 8 * g
                        sp.dma_start(q_rows[row:row + 8, :, g, :],
                                     rot[src:src + 8, part, :].rearrange("p (b t) -> p b t", b=NB)).then_inc(qk_placed, 16)
                        sp.dma_start(k_pad[row:row + 8, j, g * T:(g + 1) * T],
                                     rot[8 * g:8 * g + 8, 2 + part, :]).then_inc(qk_placed, 16)

            def place_max_rows(u):
                wait_apart(sp, mT_copied, u + 1)
                for j in range(J):
                    rows = slice(32 * j, 32 * j + MROWS)
                    sp.dma_start(q_aug[rows, ds(u, 1), :], m_T[rows, :].unsqueeze(1)).then_inc(mrow_placed, 16)

            def move_sums(u):
                wait_apart(sp, pv_copied, u + 1)
                wait(sp, inverted, u)
                for j in range(J):
                    sp.dma_start(sums[32 * j:32 * j + 32, :],
                                 heads[32 * j + HD:32 * j + HD + 1, :].rearrange("p (r c) -> p r c", c=16)).then_inc(sums_moved, 16)
                wait_apart(sp, inverted, u + 1)
                wait(sp, scale_ready, u)
                for j in range(J):
                    sp.dma_start(scale_row[32 * j:32 * j + 1, :].rearrange("p (r c) -> p r c", c=16),
                                 inv_sums[32 * j:32 * j + 32, :]).then_inc(inv_moved, 16)

            def body(b, g, mb, mg):
                if not (isinstance(g, int) and b + g == 0):
                    move_sums(g + (4 * b - 1))
                if has_next(mb, mg):
                    place_max_rows(g + (4 * b + 1))

            place_max_rows(0)
            sp.wait_ge(scale_row_set, 1)
            bodies(sp, body)
            move_sums(UNITS - 1)

            sp.wait_ge(o_done, UNITS)
            sp.sem_inc(xn2_stored, 16)
            sp.sem_inc(xn2T_all, 16)
            xn2_v = xn2_d.rearrange("(b n p) h -> p b n h", p=P, n=4)
            with sp.Fori(0, NB) as b:
                sp.wait_ge(wo_mm, b * 4 + 4)
                sp.dma_start(o_cur.rearrange("p g t -> p (g t)"),
                             o_nrm[:, ds(b * (NKV * QB), NKV * QB)]).then_inc(o_loaded, 16)
                sp.wait_ge(xn2_ready, b * 4 + 4)
                sp.dma_start(xn2_v[:, ds(b, 1), :, :].rearrange("p b n h -> p (b n) h"), xn[:, :, :]).then_inc(xn2_stored, 16)
                sp.wait_ge(xn2T_ready, b * 2 + 4)
                sp.dma_start(xn2T[:, :, ds(b * QB, QB)], xnT[:, :, :]).then_inc(xn2T_all, 16)
            sp.wait_ge(late_consts, 1)
            table_v = table_d.rearrange("(p b) w -> p (b w)", p=P)
            sp.dma_start(table_v, tab0).then_inc(table_init, 16)
            sp.wait_ge(scattered, 16 * NT * K)
            sp.dma_start(tab, table_v).then_inc(tab_loaded, 16)
            sp.wait_ge(eob_ready, 1)
            with sp.Fori(0, NBLK // 4) as it:
                for s in range(4):
                    expert = sp.value_load(eob[0:1, ds(it * 4 + s, 1)], min_val=0, max_val=E - 1)
                    sp.wait_ge(down_mm, it * 4 + (s + 1))
                    sp.dma_start(w1s[s].unsqueeze(1), w1[:, ds(expert, 1), :, :]).then_inc(w_loaded[s], 16)
                    sp.dma_start(w2s[s].unsqueeze(1), w2[:, ds(expert, 1), :, :]).then_inc(w_loaded[s], 16)
            for s in range(4):
                sp.wait_ge(y_stored[s], 16 * (NBLK // 4))
            y_t = y_d[0:DUMP, :].rearrange("(n p k) h -> p n (k h)", p=P, k=K)
            with sp.Fori(0, NT // 2) as it:
                for h in range(2):
                    sp.wait_ge(summed, it * 2 + (h + 1))
                    sp.dma_start(yk[h].unsqueeze(1), y_t[:, ds(it * 2 + h, 1), :]).then_inc(yk_loaded[h], 16)

        @block.gpsimd
        def _(gp):
            chain = Chain(gp, pool)
            chain.link(nc.gpsimd.memset(k_pad[:, :, :].rearrange("p a b -> p (a b)").bitcast(f32), 0.0))
            for j in range(J):
                chain.link(nc.gpsimd.memset(k_pad[32 * j:32 * j + MROWS, j, :], 1.0))
            gp.sem_inc(k_zeroed, 1)
            nc.gpsimd.memset(m_stage[:, :, :], 0.0)
            nc.gpsimd.memset(v_all[:, :], 16.0).then_inc(v_ones, 1)

            gp.sem_inc(rot_done, 4)
            with gp.Fori(0, NB) as b:
                for n, op in enumerate((ALU.subtract, ALU.add, ALU.subtract, ALU.add)):
                    rows = P if n < 2 else 32
                    gp.wait_ge(rot_terms, b * 8 + (2 * n + 2))
                    nc.gpsimd.tensor_tensor(rot[0:rows, n, ds(b * QB, QB)], p_ring[0:rows, 2 * n, :],
                                            p_ring[0:rows, 2 * n + 1, :], op).then_inc(rot_done, 1)

            def stage_v(b, g):
                nst, before = key_tiles(b), tiles_before(b, g)
                for st in range(nst):
                    wait_apart(gp, pv_done, before + (4 - nst + st + 1) if st < nst - 4 else before)
                    nc.gpsimd.tensor_copy(v_cur[:, st, :], v_all[:, ds(g * (NT * 32) + st * 32, 32)]).then_inc(v_staged, 1)

            def split(u):
                part = [m_stage[:, :, :].rearrange("p t (j r) -> p t j r", j=J)[:, :, :, r] for r in range(MROWS)]
                neg, r1, r2 = (t[:, :].rearrange("p (t j) -> p t j", t=4) for t in (m_neg, m_r1, m_r2))
                gp.wait_ge(max_ready, u + 1)
                wait_apart(gp, mT_ready, u)
                chain.link(nc.gpsimd.tensor_scalar(m_neg[:, :], m_row[:, :], -1.0, None, ALU.mult))
                chain.link(nc.gpsimd.tensor_copy(part[0], neg))
                chain.link(nc.gpsimd.tensor_tensor(r1, neg, part[0], ALU.subtract))
                chain.link(nc.gpsimd.tensor_copy(part[1], r1))
                chain.link(nc.gpsimd.tensor_tensor(r2, r1, part[1], ALU.subtract))
                nc.gpsimd.tensor_copy(part[2], r2).then_inc(split_done, 1)

            def normalise(u):
                gp.wait_ge(scale_ready, u + 1)
                nc.gpsimd.tensor_tensor(o_nrm[:, ds(u * QB, QB)], heads, scale, ALU.mult).then_inc(o_done, 1)

            def body(b, g, mb, mg):
                stage_v(b, g)
                if has_next(mb, mg):
                    chain.base, chain.n = g * 5 + (split_links + 5 * (4 * b + 1)), 0
                    split(g + (4 * b + 1))
                if not (isinstance(g, int) and b + g == 0):
                    normalise(g + (4 * b - 1))

            gp.wait_ge(v_done, NB + 1)
            split_links = chain.n
            split(0)
            bodies(gp, body)
            normalise(UNITS - 1)
            chain.base, chain.n = split_links + 5 * UNITS, 0
            gp.wait_ge(xn_ready, NT)
            for n in range(NT):
                nc.gpsimd.tensor_tensor(x_sb[:, n * H:(n + 1) * H], x_sb[:, n * H:(n + 1) * H], bo[:, :], ALU.add
                                        ).then_inc(xb_done, 1)

            gp.wait_ge(pv_done, tiles_before(NB - 1, NKV))
            nc.gpsimd.memset(ones_row, 1.0)
            s2 = src2.rearrange("p (n k w) -> p n k w", n=NT, k=K)
            nc.gpsimd.iota(s2[:, :, :, 0], [[P, NT], [0, K]], base=0, channel_multiplier=1)
            nc.gpsimd.iota(s2[:, :, :, 1], [[P * K, NT], [1, K]], base=0, channel_multiplier=K)
            t0 = tab0.rearrange("p (b w) -> p b w", w=2)
            nc.gpsimd.iota(t0[:, :, 0], [[0, NBLK]], base=0, channel_multiplier=0)
            nc.gpsimd.iota(t0[:, :, 1], [[P, NBLK]], base=DUMP, channel_multiplier=1).then_inc(late_consts, 1)
            gp.wait_ge(late_consts, 1)
            gp.wait_ge(table_init, 16)
            gp.wait_ge(srow_ready, 1)
            for at in range(NT * K):
                gp.indirect_dma_start(
                    out=table_d[:, :], out_offset=bass.IndirectOffsetOnAxis(ap=srow.bitcast(u32)[:, at:at + 1], axis=0),
                    in_=src2[:, 2 * at:2 * at + 2], in_offset=None).then_inc(scattered, 16)

            def gather(it, s):
                gp.wait_ge(idx_ready, it * 4 + (s + 1))
                wait_apart(gp, xg_T, it * 4 + (s + 1))
                gp.indirect_dma_start(
                    out=xg[s], out_offset=None, in_=xn2_d[:, :],
                    in_offset=bass.IndirectOffsetOnAxis(ap=ids_x[s].bitcast(u32), axis=0)).then_inc(xg_loaded[s], 16)

            def scatter(it, s):
                gp.wait_ge(idy_ready, it * 4 + (s + 1))
                wait_apart(gp, y_ready, it * 4 + (s + 3))
                gp.indirect_dma_start(
                    out=y_d[:, :], out_offset=bass.IndirectOffsetOnAxis(ap=ids_y[s].bitcast(u32), axis=0),
                    in_=ys[s], in_offset=None).then_inc(y_stored[s], 16)

            gp.wait_ge(xn2_stored, 16 * NB + 16)
            for s in range(4):
                gather(0, s)
            with gp.Fori(0, NBLK // 4 - 1) as it:
                for s in range(4):
                    gather(it + 1, s)
                    scatter(it, s)
            for s in range(4):
                scatter(NBLK // 4 - 1, s)

        @block.scalar
        def _(act):
            act.sem_inc(xnT_ready, 2)
            with act.Fori(0, NB) as b:
                act.wait_ge(xn_used, b * 4 + 8)
                act.wait_ge(v_mm, b + 1)
                for c in range(CH):
                    nc.scalar.copy(xnT[:, c, :], bank[c][:, :]).then_inc(xnT_ready, 1)

            def copy_max_rows(u):
                act.wait_ge(mT_ready, u + 1)
                wait(act, mrow_placed, u * (16 * J))
                nc.scalar.copy(m_T[:, :], bank16[7][:, 0:QB]).then_inc(mT_copied, 1)

            def body(b, g, mb, mg):
                before = tiles_before(b, g)
                for st in range(key_tiles(b)):
                    if st == key_tiles(b) - 1 and has_next(mb, mg):
                        copy_max_rows(g + (4 * b + 1))
                    at = 128 * max(0, st - 4 * b)
                    for j in range(J):
                        chunk = 4 * st + j
                        act.wait_ge(sk_ready, before * 4 + (chunk + 1))
                        if j == 0:
                            wait(act, pv_done, before + (st - 1))
                        nc.scalar.activation(p_ring[:, chunk % 8, at:QB], S_K[j % 2][:, at:QB], ACT.Exp).then_inc(p_ready, 1)
                act.wait_ge(pv_done, before + key_tiles(b))
                wait(act, o_done, g + 4 * b)
                nc.scalar.copy(heads, PV[:, :]).then_inc(pv_copied, 1)

            copy_max_rows(0)
            bodies(act, body)

            act.sem_inc(xn2T_ready, 2)
            with act.Fori(0, NB) as b:
                act.wait_ge(xn2_used, b * 4 + 8)
                act.wait_ge(logit_mm, b + 1)
                act.wait_ge(xn2T_all, b * 16 + 16)
                for c in range(CH):
                    nc.scalar.copy(xnT[:, c, :], bank[2 + c][:, :]).then_inc(xn2T_ready, 1)
                act.wait_ge(logit_sub, b + 2)
                nc.scalar.activation(ex, lg, ACT.Exp).then_inc(exp_done, 1)
            act.wait_ge(hot_mm, 1)
            for n in range(2):
                last = nc.scalar.copy(hotT[:, n * 1024:(n + 1) * 1024], bank16[6 + n][0:E, :])
            last.then_inc(hotT_done, 1)
            with act.Fori(0, NB) as b:
                for m in range(4):
                    act.wait_ge(sh_mm, b * 4 + (m + 1))
                    act.wait_ge(hs_ready, b * 4 + (m + 1))
                    nc.scalar.activation(sg[:, m % 2, :], bank[m % 2][0:HI, :], ACT.Silu).then_inc(sg_ready, 1)

            def silu(it, s):
                act.wait_ge(up_mm, it * 4 + (s + 3))
                act.wait_ge(down_mm, it * 4 + (s + 3))
                nc.scalar.activation(hT[s % 2], bank[2 + s % 2][0:HI, 0:2 * P], ACT.Silu).then_inc(h_ready, 1)

            def copy_y(it, s):
                act.wait_ge(down_mm, it * 4 + (s + 5))
                wait(act, y_stored[s], it * 16)
                nc.scalar.copy(ys[s], bank[4 + s % 2][:, 0:H]).then_inc(y_ready, 1)

            act.sem_inc(h_ready, 2)
            act.sem_inc(y_ready, 2)
            silu(0, 0)

            def silu_and_copy(it):
                for s in range(4):
                    silu(it + (s + 1) // 4, (s + 1) % 4)
                    copy_y(it, s)

            silu_and_copy(0)
            with act.Fori(1, NBLK // 4 - 1) as it:
                silu_and_copy(it)
            for s in range(4):
                if s < 3:
                    silu(NBLK // 4 - 1, s + 1)
                copy_y(NBLK // 4 - 1, s)
            for h in range(2):
                act.sem_inc(out_stored[h], 16)
            out_t = out.rearrange("o (n p) h -> p (o n) h", p=P)
            with act.Fori(0, NT // 2) as it:
                for h in range(2):
                    act.wait_ge(summed, it * 2 + (h + 3))
                    act.dma_start(out_t[:, ds(it * 2 + h, 1), :], acc[h].unsqueeze(1)).then_inc(out_stored[h], 16)
            for h in range(2):
                act.wait_ge(out_stored[h], 16 * (NT // 2) + 16)

        @block.vector
        def _(v):
            chain = Chain(v, dve)
            link = chain.link
            nc.vector.memset(q_aug[:, :, :].rearrange("p a b -> p (a b)").bitcast(f32), 0.0).then_inc(q_zeroed, 1)
            v.wait_ge(ld_c, 16)
            nc.vector.tensor_copy(ident16[:, :], ident)
            nc.vector.tensor_copy(kmask16[:, :], kmask).then_inc(consts16, 1)

            def inv_sqrt(n):
                var, y, y2, half = mv_all[:, 0:n, 1], rstd[:, 0:n], rs_tmp[:, 0, 0:n], rs_tmp[:, 1, 0:n]
                link(nc.vector.tensor_scalar(half, var, EPS, None, ALU.add))
                link(nc.vector.tensor_scalar(y2.bitcast(i32), half.bitcast(i32), 1, None, ALU.logical_shift_right))
                nc.vector.tensor_scalar(half, half, 0.5, None, ALU.mult)
                link(nc.vector.tensor_scalar(y.bitcast(i32), y2.bitcast(i32), -1.0, float(0x5F3759DF), ALU.mult, ALU.add))
                for _ in range(3):
                    link(nc.vector.scalar_tensor_tensor(y2, y, -1.0, y, ALU.mult, ALU.mult))
                    link(nc.vector.tensor_tensor(y2, y2, half, ALU.mult))
                    link(nc.vector.scalar_tensor_tensor(y, y2, 1.5, y, ALU.add, ALU.mult))

            mv_all = mv[:, :].rearrange("p (n w) -> p n w", w=2)
            for n in range(NT):
                if n % 4 == 0:
                    v.wait_ge(ld_x[n // 4], 16)
                last = nc.vector.bn_stats(stats[:, n, :], x_sb[:, n * H:(n + 1) * H])
            link(last)
            for n in range(NT):
                last = nc.vector.bn_aggr(mv[:, 2 * n:2 * n + 2], stats[:, n, :])
            link(last)
            inv_sqrt(NT)
            v.wait_ge(ld_w, 16 * 6)
            v.wait_ge(v_ones, 1)
            v_rows = v_all[:, :].rearrange("p (g m) -> p g m", g=NKV)
            v.sem_inc(v_done, 1)
            with v.Fori(0, NB) as b:
                v.wait_ge(xn_used, b * 4 + 4)
                for tt in range(4):
                    nc.vector.tensor_scalar(xn[:, tt, :], x_sb[:, ds(b * (4 * H) + tt * H, H)], mv[:, ds(b * 8 + 2 * tt, 1)],
                                            rstd[:, ds(b * 4 + tt, 1)], ALU.subtract, ALU.mult).then_inc(xn_ready, 1)
                v.wait_ge(rot_done, b * 4 + 4)
                for part, (mm, bias, rows) in enumerate(((q_mm, bq, P), (k_mm, bk, 32))):
                    even, odd = bank[2 + 2 * part][0:rows, :], bank[3 + 2 * part][0:rows, :]
                    v.wait_ge(mm, b + 1)
                    for n, (src, w, tabl) in enumerate(((even, 0, cos), (odd, 1, sin), (even, 0, sin), (odd, 1, cos))):
                        nc.vector.scalar_tensor_tensor(p_ring[0:rows, 4 * part + n, :], src, bias[0:rows, w:w + 1],
                                                       tabl[0:rows, ds(b * QB, QB)], ALU.add, ALU.mult).then_inc(rot_terms, 1)
                v.wait_ge(v_mm, b + 2)
                v_ps = bank[6][:, 0:4 * NKV * HD].rearrange("p (n g d) -> p n g d", n=4, g=NKV)
                bv_g = bv[:, :].rearrange("p (g d) -> p g d", g=NKV)
                for tt in range(4):
                    last = nc.vector.tensor_tensor(v_rows[:, :, ds(b * 128 + tt * 32, HD)], v_ps[:, tt, :, :], bv_g, ALU.add)
                last.then_inc(v_done, 1)

            nc.vector.memset(scale_row, 1.0).then_inc(scale_row_set, 1)

            def row_max(b, g, n):
                tt, c, j = max_chunks(b)[n]
                src = S_Q[n % 4]
                at = m_part[:, tt * J + j, c:c + 1]
                (v.wait_ge if c < b else lambda *a: wait_apart(v, *a))(sq_ready, maxes_before(b, g) + (n + 1))
                if c < b:
                    nc.vector.reduce_max(at, src[:, :], AX.X).then_inc(sq_used, 1)
                else:
                    w = 128 * (tt + 1)
                    nc.vector.tensor_tensor_reduce(out=src[:, 0:w], in0=src[:, 0:w], in1=qmask[:, 512 - w:512], scale=1.0,
                                                   scalar=-3.0e38, op0=ALU.add, op1=ALU.max, accum_out=at).then_inc(sq_used, 1)

            def row_max_all(b, g, u, between=None):
                wait_apart(v, max_ready, u)
                for n in range(16 * (b + 1)):
                    row_max(b, g, n)
                    if between:
                        between(n + 1)
                v.wait_ge(sq_used, maxes_before(b, g) + 16 * (b + 1))
                wait(v, split_done, u)
                nc.vector.reduce_max(m_row[:, :], m_part[:, :, 0:b + 1], AX.X).then_inc(max_ready, 1)

            def invert_sums(u):
                v.wait_ge(sums_moved, (u + 1) * (16 * J))
                nc.vector.reciprocal(inv_sums[:, :], sums[:, :]).then_inc(inverted, 1)

            def spread_scale(u):
                v.wait_ge(inv_moved, (u + 1) * (16 * J))
                wait_apart(v, o_done, u)
                nc.vector.stream_shuffle(scale, scale_row, [0] * 32).then_inc(scale_ready, 1)

            def body(b, g, mb, mg):
                def between(n):
                    if n == 8:
                        invert_sums(g + (4 * b - 1))
                    if n == 16:
                        spread_scale(g + (4 * b - 1))

                if isinstance(g, int) and b + g == 0:
                    between = None
                if mb is not None:
                    row_max_all(mb, mg, g + (4 * b + 2), between)
                else:
                    between(8)
                    between(16)

            row_max_all(0, 0, 0)
            row_max_all(0, 1, 1)
            bodies(v, body)
            invert_sums(UNITS - 1)
            spread_scale(UNITS - 1)

            v.wait_ge(xb_done, NT)
            v.sem_inc(x1_done, 2)
            v.sem_inc(logit_sub, 1)
            v4 = lambda t: t.rearrange("p (n e) -> p n e", n=4)
            with v.Fori(0, NB) as b:
                chain.enter(b, 25)
                v.wait_ge(xn2_used, b * 4 + 4)
                v.wait_ge(xn2_stored, b * 16 + 16)
                for tt in range(4):
                    xs = x_sb[:, ds(b * (4 * H) + tt * H, H)]
                    v.wait_ge(wo_mm, b * 4 + (tt + 5))
                    nc.vector.tensor_tensor(xs, bank[tt % 2][:, 0:H], xs, ALU.add).then_inc(x1_done, 1)
                wait_apart(v, x1_done, b * 4 + 6)
                for tt in range(4):
                    last = nc.vector.bn_stats(stats[:, tt, :], x_sb[:, ds(b * (4 * H) + tt * H, H)])
                link(last)
                for tt in range(4):
                    last = nc.vector.bn_aggr(mv[:, 2 * tt:2 * tt + 2], stats[:, tt, :])
                link(last)
                inv_sqrt(4)
                for tt in range(4):
                    nc.vector.tensor_scalar(xn[:, tt, :], x_sb[:, ds(b * (4 * H) + tt * H, H)], mv[:, 2 * tt:2 * tt + 1],
                                            rstd[:, tt:tt + 1], ALU.subtract, ALU.mult).then_inc(xn2_ready, 1)
                v.wait_ge(logit_mm, b + 2)
                logits = v4(bank[4][:, 0:4 * E])
                link(nc.vector.reduce_max(row4, logits, AX.X))
                nc.vector.tensor_tensor(v4(lg), logits, row4.unsqueeze(2).to_broadcast([P, 4, E]), ALU.subtract
                                        ).then_inc(logit_sub, 1)
                v.wait_ge(exp_done, b + 1)
                link(nc.vector.reduce_sum(sum4, v4(ex), AX.X))
                link(nc.vector.reciprocal(sum4, sum4))
                link(nc.vector.tensor_tensor(v4(pr), v4(ex), sum4.unsqueeze(2).to_broadcast([P, 4, E]), ALU.mult))
                for tt in range(4):
                    last = nc.vector.max(top8[:, 8 * tt:8 * tt + 8], pr[:, E * tt:E * tt + E])
                link(last)
                for tt in range(4):
                    last = nc.vector.max_index(idx8[:, 8 * tt:8 * tt + 8], top8[:, 8 * tt:8 * tt + 8], pr[:, E * tt:E * tt + E])
                link(last)
                link(nc.vector.reduce_sum(sum6, v4(top8)[:, :, 0:K], AX.X))
                link(nc.vector.reciprocal(sum6, sum6))
                link(nc.vector.tensor_tensor(wts[:, ds(b * (4 * K), 4 * K)].rearrange("p (n k) -> p n k", n=4), v4(top8)[:, :, 0:K],
                                             sum6.unsqueeze(2).to_broadcast([P, 4, K]), ALU.mult))
                link(nc.vector.tensor_copy(idxf, idx8))
                for tt in range(4):
                    last = nc.vector.tensor_tensor(
                        hot[:, ds(b * (4 * K * E) + tt * K * E, K * E)].rearrange("p (k e) -> p k e", k=K),
                        iota_e.unsqueeze(1).to_broadcast([P, K, E]),
                        idxf[:, 8 * tt:8 * tt + K].unsqueeze(2).to_broadcast([P, K, E]), ALU.is_equal)
                link(last)
                with nc.allow_low_precision("sums of six zeros and ones"):
                    nc.vector.reduce_sum(chosen[:, ds(b * (4 * E), 4 * E)].rearrange("p (n e) -> p n e", n=4),
                                              hot[:, ds(b * (4 * K * E), 4 * K * E)].rearrange("p (n k e) -> p n e k", n=4, k=K), AX.X).then_inc(chosen_ready, 1)
                chain.leave(NB)

            v.wait_ge(hotT_done, 1)
            v.wait_ge(late_consts, 1)
            link(nc.vector.tensor_tensor_scan(cum, ones_row, hotT, 0.0, ALU.mult, ALU.add))
            c_int = cnt.bitcast(i32)
            link(nc.vector.tensor_scalar(c_int[:, 0:1], cum[:, T - 1:T], float(P - 1), None, ALU.add))
            link(nc.vector.tensor_scalar(c_int[:, 1:2], c_int[:, 0:1], -P, None, ALU.bitwise_and))
            nc.vector.tensor_copy(cnt[:, 2:3], c_int[:, 1:2]).then_inc(padded, 1)
            v.wait_ge(base_mm, 1)
            nc.vector.tensor_copy(cnt[:, 4:5], bank[5][0:E, 1:2])
            link(nc.vector.tensor_scalar(cnt[:, 3:4], bank[5][0:E, 0:1], -1.0, None, ALU.add))
            nc.vector.tensor_scalar(past_end, blk_start, cnt[:, 4:5], None, ALU.is_ge).then_inc(past_ready, 1)
            nc.vector.tensor_scalar(cum, cum, cnt[:, 3:4], None, ALU.add).then_inc(slotT_ready, 1)
            for n in range(2):
                v.wait_ge(slotT_mm, n + 1)
                hv = hot[:, n * 8 * K * E:(n + 1) * 8 * K * E].rearrange("p (n k e) -> p n k e", n=8, k=K)
                sv = bank[6 + n][:, :].rearrange("p (n e) -> p n e", n=8)
                for t in range(8):
                    last = nc.vector.tensor_tensor(prod.rearrange("p (n k e) -> p n k e", n=8, k=K)[:, t, :, :], hv[:, t, :, :],
                                                   sv[:, t, :].unsqueeze(1).to_broadcast([P, K, E]), ALU.mult)
                link(last)
                link(nc.vector.reduce_sum(slot[:, n * 8 * K:(n + 1) * 8 * K].rearrange("p (n k) -> p n k", k=K),
                                          prod.rearrange("p (n k e) -> p n k e", n=8, k=K), AX.X))
            link(nc.vector.tensor_copy(slot_i, slot))
            nc.vector.tensor_scalar(smod, slot_i, P - 1, None, ALU.bitwise_and)
            link(nc.vector.tensor_scalar(sdiv, slot_i, 7, None, ALU.logical_shift_right))
            nc.vector.scalar_tensor_tensor(srow, smod, float(NBLK), sdiv, ALU.mult, ALU.add).then_inc(srow_ready, 1)
            v.wait_ge(eob_mm, 1)
            link(nc.vector.tensor_scalar(past_end[0:1, :], bank[5][0:1, 2:2 + NBLK], float(E - 1), None, ALU.min))
            nc.vector.tensor_copy(eob, past_end[0:1, :]).then_inc(eob_ready, 1)

            v.sem_inc(hs_ready, 2)
            v.sem_inc(sh_added, 2)
            with v.Fori(0, NB) as b:
                v.wait_ge(shd_mm, b * 4 + 4)
                for m in range(4):
                    v.wait_ge(sg_ready, b * 4 + (m + 1))
                    nc.vector.tensor_tensor(hs[:, m, :], bank[2 + m % 2][0:HI, :], sg[:, m % 2, :], ALU.mult).then_inc(hs_ready, 1)
                for tt in range(4):
                    xs = x_sb[:, ds(b * (4 * H) + tt * H, H)]
                    v.wait_ge(shd_mm, b * 4 + (tt + 5))
                    nc.vector.tensor_tensor(xs, bank[4 + tt % 2][:, 0:H], xs, ALU.add).then_inc(sh_added, 1)

            def stage_x(it, s):
                nc.vector.tensor_copy(ids_x[s], tab[:, ds((it * 4 + s) * 2, 1)]).then_inc(idx_ready, 1)

            def rows_T(it, s):
                v.wait_ge(xg_T, it * 4 + (s + 5))
                v.wait_ge(up_mm, it * 4 + (s + 1))
                nc.vector.tensor_copy(xgT[s % 2], bank[s % 2][:, 0:H]).then_inc(xgT_ready, 1)
                wait(v, y_stored[s], it * 16)
                nc.vector.tensor_copy(ids_y[s], tab[:, ds((it * 4 + s) * 2 + 1, 1)]).then_inc(idy_ready, 1)

            v.wait_ge(tab_loaded, 16)
            for s in range(4):
                stage_x(0, s)
            v.sem_inc(xgT_ready, 2)

            def four_blocks(it):
                for s in range(4):
                    rows_T(it, s)
                    stage_x(it + 1, s)

            four_blocks(0)
            with v.Fori(1, NBLK // 4 - 1) as it:
                four_blocks(it)
            for s in range(4):
                rows_T(NBLK // 4 - 1, s)

            v.sem_inc(summed, 2)
            with v.Fori(0, NT // 2) as it:
                chain.enter(it, 2 * (K - 1))
                for h in range(2):
                    v.wait_ge(yk_loaded[h], it * 16 + 16)
                    v.wait_ge(out_stored[h], it * 16 + 16)
                    for k in range(K):
                        prev = x_sb[:, ds(it * (2 * H) + h * H, H)] if k == 0 else acc[h]
                        ins = nc.vector.scalar_tensor_tensor(acc[h], yk[h][:, k * H:(k + 1) * H],
                                                             wts[:, ds(it * (2 * K) + (h * K + k), 1)], prev, ALU.mult, ALU.add)
                        if k < K - 1:
                            link(ins)
                        else:
                            ins.then_inc(summed, 1)
                chain.leave(NT // 2)

        @block.tensor
        def _(pe):
            def mm(o, lhsT, rhs, first=True, last=True):
                return nc.tensor.matmul(o, lhsT, rhs, start=first, stop=last)

            pe.wait_ge(ld_c, 16)
            pe.wait_ge(ld_w, 16 * 6)
            pe.sem_inc(xn_used, 4)
            pe.sem_inc(v_mm, 1)
            with pe.Fori(0, NB) as b:
                pe.wait_ge(xnT_ready, b * 2 + 2)
                for tt in range(4):
                    pe.wait_ge(xn_ready, b * 4 + (tt + 1))
                    for c in range(CH):
                        last = nc.tensor.transpose(bank[c][:, tt * P:(tt + 1) * P], xn[:, tt, c * P:(c + 1) * P], ident)
                    last.then_inc(xn_used, 1)
                pe.wait_ge(xnT_ready, b * 2 + 4)
                pe.wait_ge(v_done, b + 1)
                cols = ((2, 0, P, q_mm), (3, P, P, q_mm), (4, 2 * P, 32, k_mm), (5, 2 * P + 32, 32, k_mm))
                for n, (bk_n, at, m, done) in enumerate(cols):
                    for c in range(CH):
                        last = mm(bank[bk_n][0:m, :], wqkv[:, c, at:at + m], xnT[:, c, :], c == 0, c == CH - 1)
                    if n % 2:
                        last.then_inc(done, 1)
                for tt in range(4):
                    for c in range(CH):
                        last = mm(bank[6][:, tt * 64:(tt + 1) * 64], xnT[:, c, tt * P:(tt + 1) * P],
                                  wqkv[:, c, 320:384], c == 0, c == CH - 1)
                last.then_inc(v_mm, 1)

            def score_q(b, g, n):
                tt, c, j = max_chunks(b)[n]
                w = QB if c < b else 128 * (tt + 1)
                before = maxes_before(b, g)
                wait(pe, sq_used, before + (n - 3))
                mm(S_Q[n % 4][:, 0:w], q_aug[:, ds(g + 4 * b, 1), tt * P:(tt + 1) * P].rearrange("p u t -> p (u t)"),
                   k_pad[:, j, ds(g * T + c * QB, w)]).then_inc(sq_ready, 1)

            def score_k(b, g, st, j):
                n, before = 4 * st + j, tiles_before(b, g)
                at = 128 * max(0, st - 4 * b)
                diagonal = st >= 4 * b
                wait(pe, p_ready, before * 4 + (n - 1))
                o = S_K[j % 2]
                last = mm(o[:, at:QB], k_pad[:, j, ds(g * T + st * P, P)],
                          q_aug[:, ds(g + 4 * b, 1), at:QB].rearrange("p u t -> p (u t)"), True, not diagonal)
                if diagonal:
                    last = mm(o[:, at:at + P], ident16[:, :], kmask16[:, :], False, True)
                last.then_inc(sk_ready, 1)

            def p_times_v(b, g, st):
                before = tiles_before(b, g)
                at = 128 * max(0, st - 4 * b)
                pe.wait_ge(p_ready, before * 4 + (4 * st + 4))
                pe.wait_ge(v_staged, before + (st + 1))
                if st == 0:
                    wait(pe, pv_copied, g + 4 * b)
                for j in range(J):
                    last = mm(PV[32 * j:32 * j + 32, at:QB], v_cur[:, st, :], p_ring[:, (4 * st + j) % 8, at:QB],
                              st == 0, st == key_tiles(b) - 1)
                last.then_inc(pv_done, 1)

            def transpose_max(u):
                pe.wait_ge(split_done, u + 1)
                wait(pe, mT_copied, u)
                for tt in range(4):
                    last = nc.tensor.transpose(bank16[7][:, tt * P:(tt + 1) * P], m_stage[:, tt, :], ident16[:, :])
                last.then_inc(mT_ready, 1)

            def body(b, g, mb, mg):
                nst = key_tiles(b)
                n_max = 16 * (mb + 1) if mb is not None else 0
                pe.wait_ge(mrow_placed, g * (16 * J) + (4 * b + 1) * 16 * J)
                for st in range(nst):
                    if st == nst - 2 and has_next(mb, mg):
                        transpose_max(g + (4 * b + 1))
                    todo = list(range(n_max * st // nst, n_max * (st + 1) // nst))
                    for j in range(J):
                        for n in todo[len(todo) * j // J:len(todo) * (j + 1) // J]:
                            score_q(mb, mg, n)
                        score_k(b, g, st, j)
                    if st:
                        p_times_v(b, g, st - 1)
                p_times_v(b, g, nst - 1)

            pe.wait_ge(consts16, 1)
            pe.wait_ge(qk_placed, 16 * 4 * NKV * J)
            for g in range(2):
                for n in range(16):
                    score_q(0, g, n)
            transpose_max(0)
            bodies(pe, body)

            pe.wait_ge(ld_late, 16 * 4)
            pe.wait_ge(o_done, UNITS)
            pe.sem_inc(wo_mm, 4)
            pe.sem_inc(xn2_used, 4)
            pe.sem_inc(logit_mm, 1)
            with pe.Fori(0, NB) as b:
                pe.wait_ge(o_loaded, b * 16 + 16)
                for tt in range(4):
                    pe.wait_ge(x1_done, b * 4 + (tt + 1))
                    for g in range(NKV):
                        last = mm(bank[tt % 2][:, 0:H], o_cur[:, g, tt * P:(tt + 1) * P], wo[:, g, :], g == 0, g == NKV - 1)
                    last.then_inc(wo_mm, 1)
                pe.wait_ge(xn2T_ready, b * 2 + 2)
                for tt in range(4):
                    pe.wait_ge(xn2_ready, b * 4 + (tt + 1))
                    for c in range(CH):
                        last = nc.tensor.transpose(bank[2 + c][:, tt * P:(tt + 1) * P], xn[:, tt, c * P:(c + 1) * P], ident)
                    last.then_inc(xn2_used, 1)
                pe.wait_ge(xn2T_ready, b * 2 + 4)
                pe.wait_ge(logit_sub, b + 1)
                for tt in range(4):
                    for c in range(CH):
                        last = mm(bank[4][:, tt * E:(tt + 1) * E], xnT[:, c, tt * P:(tt + 1) * P], gate_sb[:, c, :],
                                  c == 0, c == CH - 1)
                last.then_inc(logit_mm, 1)

            pe.wait_ge(chosen_ready, NB)
            for n in range(NT):
                last = nc.tensor.transpose(bank16[6 + n // 8][0:E, n % 8 * P:(n % 8 + 1) * P], chosen[:, n * E:(n + 1) * E], ident16[:, :])
            last.then_inc(hot_mm, 1)
            pe.wait_ge(padded, 1)
            mm(bank[5][0:E, 0:1], tri_before, cnt[:, 2:3])
            mm(bank[5][0:E, 1:2], tri_upto, cnt[:, 2:3]).then_inc(base_mm, 1)
            pe.wait_ge(past_ready, 1)
            mm(bank[5][0:1, 2:2 + NBLK], ones_col, past_end).then_inc(eob_mm, 1)
            pe.wait_ge(slotT_ready, 1)
            for n in range(NT):
                last = nc.tensor.transpose(bank[6 + n // 8][:, n % 8 * E:(n % 8 + 1) * E], cum[:, n * P:(n + 1) * P], ident[0:E, 0:E])
                if n % 8 == 7:
                    last.then_inc(slotT_mm, 1)
            pe.wait_ge(xn2T_all, 16 * NB + 16)
            pe.wait_ge(eob_ready, 1)
            pe.sem_inc(shd_mm, 4)
            with pe.Fori(0, NB) as b:
                for m in range(4):
                    pe.wait_ge(hs_ready, b * 4 + (m + 1))
                    for half in range(2):
                        at = half * SI + m * HI
                        for c in range(CH):
                            last = mm(bank[2 * half + m % 2][0:HI, :], sh1[:, c, at:at + HI], xn2T[:, c, ds(b * QB, QB)],
                                      c == 0, c == CH - 1)
                    last.then_inc(sh_mm, 1)
                pe.wait_ge(hs_ready, b * 4 + 6)
                for tt in range(4):
                    pe.wait_ge(sh_added, b * 4 + (tt + 1))
                    for m in range(4):
                        last = mm(bank[4 + tt % 2][:, 0:H], hs[:, m, tt * P:(tt + 1) * P], sh2[:, m, :], m == 0, m == 3)
                    last.then_inc(shd_mm, 1)

            def rows_T(it, s):
                pe.wait_ge(xg_loaded[s], it * 16 + 16)
                pe.wait_ge(xgT_ready, it * 4 + (s + 1))
                for c in range(CH):
                    last = nc.tensor.transpose(bank[s % 2][:, c * P:(c + 1) * P], xg[s][:, c * P:(c + 1) * P], ident)
                last.then_inc(xg_T, 1)

            def up(it, s):
                pe.wait_ge(w_loaded[s], it * 32 + 32)
                pe.wait_ge(xgT_ready, it * 4 + (s + 3))
                pe.wait_ge(h_ready, it * 4 + (s + 1))
                for i in range(2):
                    for c in range(CH):
                        last = mm(bank[2 + s % 2][0:HI, i * P:(i + 1) * P], w1s[s][:, c, i * HI:(i + 1) * HI],
                                  xgT[s % 2][:, c * P:(c + 1) * P], c == 0, c == CH - 1)
                last.then_inc(up_mm, 1)

            def down(it, s):
                pe.wait_ge(h_ready, it * 4 + (s + 3))
                pe.wait_ge(y_ready, it * 4 + (s + 1))
                for i in range(2):
                    last = mm(bank[4 + s % 2][:, 0:H], hT[s % 2][:, i * P:(i + 1) * P], w2s[s][:, i, :], i == 0, i == 1)
                last.then_inc(down_mm, 1)

            pe.wait_ge(sh_added, NT + 2)
            pe.sem_inc(xg_T, 4)
            pe.sem_inc(up_mm, 2)
            pe.sem_inc(down_mm, 4)
            rows_T(0, 0)
            rows_T(0, 1)
            up(0, 0)
            with pe.Fori(0, NBLK // 4 - 1) as it:
                for s in range(4):
                    rows_T(it + (s + 2) // 4, (s + 2) % 4)
                    up(it + (s + 1) // 4, (s + 1) % 4)
                    down(it, s)
            end = NBLK // 4 - 1
            for s in range(4):
                if s < 2:
                    rows_T(end, s + 2)
                if s < 3:
                    up(end, s + 1)
                down(end, s)


_INS = ["x", "w_qkv", "b_q", "b_k", "b_v", "b_o", "w_o", "gate", "w_sh1", "w_sh2", "w1", "w2", "trig", "cst"]


def constants():
    freqs = (np.float32(10000.0) ** -(np.arange(0, H, 2, dtype=np.float32) / np.float32(H)))[:HD // 2]
    ang = np.outer(freqs, np.arange(T, dtype=np.float32)).astype(np.float32)
    rows = np.tile(ang.astype(np.float64), (P // (HD // 2), 1))
    trig = np.concatenate([np.cos(rows), np.sin(rows)], axis=1).astype(np.float32)
    p, c = np.arange(P)[:, None], np.arange(512)[None, :]
    cst = np.zeros((P, 1121), np.float32)
    cst[:, 0:128] = np.eye(P)
    cst[:, 128:640] = np.where(c <= 384 + p, 0.0, BIG)
    cst[:, 640:768] = np.where(c[:, :P] >= p, 0.0, BIG)
    cst[:, 768:832] = np.arange(E)
    cst[:, 832:896] = p < c[:, :E]
    cst[:, 896:960] = p <= c[:, :E]
    cst[:, 960:1120] = np.arange(NBLK) * P
    cst[:, 1120] = 1.0
    return trig, cst


def laid_out(a):
    def chunks(w, rows):
        return w.reshape(-1, rows, w.shape[-1]).transpose(1, 0, 2)

    def q_cols(w):
        w = w.reshape(-1, NKV, J, HD // 2, 2).transpose(0, 2, 1, 3, 4)
        return [w[..., n].reshape(w.shape[0], -1) for n in range(2)]

    def k_cols(w):
        w = w.reshape(-1, NKV, HD // 2, 2)
        return [w[..., n].reshape(w.shape[0], -1) for n in range(2)]

    qe, qo = q_cols(a["L0_attn_Wq"])
    ke, ko = k_cols(a["L0_attn_Wk"])
    bqe, bqo = q_cols(a["L0_attn_bq"][None, :])
    bke, bko = k_cols(a["L0_attn_bk"][None, :])
    wo = np.zeros((J, 32, NKV, H), np.float32)
    wo[:, :HD] = a["L0_attn_Wo"].reshape(NKV, J, HD, H).transpose(1, 2, 0, 3)
    trig, cst = constants()
    return {
        "x": a["L0_attn_x"],
        "w_qkv": chunks(np.concatenate([qe, qo, ke, ko, a["L0_attn_Wv"]], axis=1), P),
        "b_q": np.stack([bqe[0], bqo[0]], axis=1),
        "b_k": np.stack([bke[0], bko[0]], axis=1),
        "b_v": np.broadcast_to(a["L0_attn_bv"], (P, NKV * HD)),
        "b_o": np.broadcast_to(a["L0_attn_bo"], (P, H)),
        "w_o": wo.reshape(P, NKV, H),
        "gate": chunks(a["L0_ffn_gate_w"].T, P),
        "w_sh1": chunks(a["L0_ffn_shared_gate_up"].T, P),
        "w_sh2": chunks(a["L0_ffn_shared_down"].T, HI),
        "w1": a["L0_ffn_experts_w1"].reshape(E, I, CH, P).transpose(3, 0, 2, 1),
        "w2": a["L0_ffn_experts_w2"].reshape(E, H, 2, HI).transpose(3, 0, 2, 1),
        "trig": trig,
        "cst": cst,
    }


def kernel(**inputs):
    import concourse.bacc as _bacc
    from concourse.bass_utils import run_bass_kernel_spmd as _run

    arrays = {f"in_{k}": np.ascontiguousarray(v) for k, v in laid_out({k: np.asarray(v) for k, v in inputs.items()}).items()}
    nc = _bacc.Bacc("TRN2", target_bir_lowering=False, num_devices=1)
    args = [nc.dram_tensor(f"in_{n}", arrays[f"in_{n}"].shape, mybir.dt.from_np(arrays[f"in_{n}"].dtype),
                           kind="ExternalInput").ap() for n in _INS]
    out = nc.dram_tensor("out", (1, T, H), mybir.dt.float32, kind="ExternalOutput").ap()
    preln_attention_moe(nc, *args, out)
    r = _run(nc, [arrays], core_ids=[0])
    return r.results[0]["out"]
```

```python
import concourse.bass as bass
from concourse import mybir
from contextlib import ExitStack
import numpy as np

T, H = 2048, 256
NH, NKV, HD = 16, 4, 16
E, I, K = 64, 176, 6
SI = 2 * I
P = 128
NT = T // P
QB = 512
NB = T // QB
J = NH // NKV
HI = I // 2
CH = H // P
UNITS = NB * NKV
MROWS = 3
NBLK = 160
SLOTS = NBLK * P
STEP = 8
ROWS = T * K
RW = H + 1
EPS = 1e-5
BIG = -1.0e30


def preln_attention_moe(nc, x, w_qkv, b_q, b_k, b_v, b_o, w_o, gate, w_sh1, w_sh2, w1, w2, trig, cst, out):
    f32, bf16, i32, u32 = mybir.dt.float32, mybir.dt.bfloat16, mybir.dt.int32, mybir.dt.uint32
    ALU, ACT, AX = mybir.AluOpType, mybir.ActivationFunctionType, mybir.AxisListType
    ds = bass.ds

    q_d = nc.dram_tensor("rotated_q", [NB, J, NKV, HD, QB], bf16).ap()
    k_d = nc.dram_tensor("rotated_k", [NB, NKV, HD, QB], bf16).ap()
    xs_d = nc.dram_tensor("slot_rows", [SLOTS, RW], f32).ap()
    y_d = nc.dram_tensor("expert_rows", [ROWS, H], f32).ap()

    ctx = ExitStack()
    with ctx:
        def sb(name, shape, dt=f32):
            return ctx.enter_context(nc.sbuf_tensor(name, shape, dt))

        def sem(name):
            return ctx.enter_context(nc.semaphore(name))

        x_sb = sb("x_sb", [P, NT * H])
        wqkv = sb("wqkv", [P, CH, 384])
        bq, bk = sb("bq", [P, 2]), sb("bk", [32, 2])
        bv, bo = sb("bv", [P, NKV * HD]), sb("bo", [P, H])
        wo = sb("wo", [P, NKV, H])
        gate_sb = sb("gate_sb", [P, CH, E])
        sh1 = sb("sh1", [P, CH, 2 * SI])
        sh2 = sb("sh2", [HI, 4, H])
        c_sb = sb("c_sb", [P, cst.shape[1]])
        ident = c_sb[:, 0:128]
        qmask = c_sb[:, 128:640]
        kmask = c_sb[:, 640:768]
        iota_e = c_sb[:, 768:832]
        tri_before = c_sb[0:E, 832:896]
        tri_upto = c_sb[0:E, 896:960]
        blk_start = c_sb[0:E, 960:960 + NBLK]
        ones_col = c_sb[0:E, 1120:1121]
        zero = sb("zero", [P, 1])
        ident16 = sb("ident16", [P, P], bf16)
        kmask16 = sb("kmask16", [P, P], bf16)
        stats = sb("stats", [P, NT, 6])
        mv = sb("mv", [P, NT * 2])
        rstd = sb("rstd", [P, NT])
        rs_tmp = sb("rs_tmp", [P, 2, NT])
        xn = sb("xn", [P, 4, H])
        xnT = sb("xnT", [P, CH, QB])
        q_aug = sb("q_aug", [P, UNITS, QB], bf16)
        k_pad = sb("k_pad", [P, J, NKV * T], bf16)
        v_all = sb("v_all", [P, NKV * NT * 32])
        v_cur = sb("v_cur", [P, NT, 32])
        p_ring = sb("p_ring", [P, 8, QB])
        o_nrm = sb("o_nrm", [P, UNITS * QB])
        cos, sin = o_nrm[:, 0:T], o_nrm[:, T:2 * T]
        rot = o_nrm[:, 2 * T:4 * T].bitcast(bf16).rearrange("p (a t) -> p a t", a=4)
        xn2T = sb("xn2T", [P, CH, T])
        m_part = sb("m_part", [P, 16, NB])
        m_row, m_neg, m_r1, m_r2 = sb("m_row", [P, 16]), sb("m_neg", [P, 16]), sb("m_r1", [P, 16]), sb("m_r2", [P, 16])
        m_stage = sb("m_stage", [P, 4, P], bf16)
        m_T = sb("m_T", [P, QB], bf16)
        xn_flat = xn[:, :, :].rearrange("p n h -> p (n h)")
        scale, fill = xn_flat[:, 0:QB], xn_flat[:, QB:QB + RW]
        heads, scale_row = xnT[:, 0, :], xnT[:, 1, :]
        sums, inv_sums = sb("sums", [P, 16]), sb("inv_sums", [P, 16])
        places = {"k_pad": [k_pad[:, :, :].rearrange("p a b -> p (a b)").bitcast(f32), 0, J * NKV * T // 2],
                  "o_nrm": [o_nrm[:, :], 0, UNITS * QB],
                  "p_ring": [p_ring[:, :, :].rearrange("p a b -> p (a b)"), 0, 8 * QB],
                  "q_aug": [q_aug[:, :, :].rearrange("p a b -> p (a b)").bitcast(f32), 0, UNITS * QB // 2]}

        def lt(n, dt=f32, rows=P, where="k_pad"):
            ap, at, size = places[where]
            places[where][1] += n
            assert at + n <= size, where
            return ap[0:rows, at:at + n] if dt == f32 else ap[0:rows, at:at + n].bitcast(dt)

        hs = lt(4 * QB, rows=HI).rearrange("p (m t) -> p m t", m=4)
        hot = lt(NT * K * E // 2, bf16)
        chosen = lt(NT * E // 2, bf16)
        cum, spare, ones_row = lt(T, rows=E), lt(T), lt(T, rows=E)
        hotT = spare[0:E, :]
        stage = [lt(K * RW, where="o_nrm").rearrange("p (k w) -> p k w", k=K) for _ in range(2)]
        prod = o_nrm[:, 0:NT * K * E // 2]
        xn2_all = p_ring[:, :, :].rearrange("p a b -> p (a b)")
        lg = [xn_flat[:, h * 8 * E:(h + 1) * 8 * E] for h in range(2)]
        ex = [xnT[:, h, :] for h in range(2)]
        pr = lt(8 * E)
        row8, sum8, sum6 = [lt(8) for _ in range(2)], lt(8), lt(8)
        top8, idx8, idxf = lt(64), lt(64, u32), lt(64)
        wts = lt(NT * K)
        slot, slot_i = lt(NT * K), lt(NT * K, i32)
        row_i, row_f = lt(NT * K, i32), lt(NT * K)
        cnt = lt(8, rows=E)
        past_end = lt(NBLK, rows=E)
        eob = lt(NBLK, i32, rows=1)
        sg = lt(2 * QB, rows=HI).rearrange("p (a t) -> p a t", a=2)
        w1s = [lt(CH * I, where="q_aug").rearrange("p (c i) -> p c i", c=CH) for _ in range(4)]
        w2s = [lt(2 * H, rows=HI, where="q_aug").rearrange("p (c n) -> p c n", c=2) for _ in range(4)]
        ids_y = [lt(1, i32) for _ in range(STEP)]
        xg, ys = [lt(RW, where="o_nrm") for _ in range(STEP)], [spare[:, n * H:(n + 1) * H] for n in range(STEP)]
        xgT = [lt(H, where="o_nrm") for _ in range(2)]
        hT = [lt(2 * P, rows=HI, where="o_nrm") for _ in range(2)]
        yk = [o_nrm[:, n * K * H:(n + 1) * K * H] for n in range(4)]
        acc = [o_nrm[:, 4 * K * H + n * H:4 * K * H + (n + 1) * H] for n in range(4)]

        bank = [ctx.enter_context(nc.psum_tensor(f"bank{n}", [P, 512], f32)) for n in range(8)]
        bank16 = [b[:, :].bitcast(bf16) for b in bank]
        S_Q = bank[0:4]
        S_K = bank[4:6]
        PV = bank[6]

        passed = sem("passed")
        ld_x = [sem(f"ld_x{n}") for n in range(4)]
        (ld_w, ld_qkv, k_ones, rot_stored, zero_set, ld_c, ld_late, consts16, q_zeroed, k_zeroed, v_ones, dve, pool) = map(sem, (
            "ld_w", "ld_qkv", "k_ones", "rot_stored", "zero_set", "ld_c", "ld_late", "consts16", "q_zeroed", "k_zeroed", "v_ones", "dve_chain", "pool_chain"))
        (xn_ready, xn_used, xnT_ready, q_mm, k_mm, v_mm, rot_terms, rot_done, qk_placed, v_done) = map(sem, (
            "xn_ready", "xn_used", "xnT_ready", "q_mm", "k_mm", "v_mm", "rot_terms", "rot_done",
            "qk_placed", "v_done"))
        (sq_ready, sq_used, sk_ready, p_ready, pv_done, v_staged, max_ready, split_done, mT_ready, mT_copied,
         mrow_placed, o_done, pv_copied, sums_moved, inverted, inv_moved, scale_ready,
         scale_row_set, xb_done) = map(sem, (
            "sq_ready", "sq_used", "sk_ready", "p_ready", "pv_done", "v_staged", "max_ready", "split_done",
            "mT_ready", "mT_copied", "mrow_placed", "o_done", "pv_copied", "sums_moved", "inverted",
            "inv_moved", "scale_ready", "scale_row_set", "xb_done"))
        (wo_mm, x1_done, xn2_ready, xn2_used, xn2T_ready, logit_mm, logit_sub,
         exp_done, chosen_ready) = map(sem, (
            "wo_mm", "x1_done", "xn2_ready", "xn2_used", "xn2T_ready",
            "logit_mm", "logit_sub", "exp_done", "chosen_ready"))
        (hot_mm, hotT_done, late_consts, padded, base_mm, slotT_ready, slotT_mm, past_ready, eob_mm,
         eob_ready, slot_ready, filled, fill_set, staged) = map(sem, (
            "hot_mm", "hotT_done", "late_consts", "padded", "base_mm", "slotT_ready", "slotT_mm",
            "past_ready", "eob_mm", "eob_ready", "slot_ready", "filled", "fill_set", "staged"))
        scattered = [sem(f"scattered{n}") for n in range(2)]
        (sh_mm, sg_ready, hs_ready, shd_mm, sh_added) = map(sem, (
            "sh_mm", "sg_ready", "hs_ready", "shd_mm", "sh_added"))
        w_loaded = [sem(f"w_loaded{n}") for n in range(4)]
        xg_loaded = [sem(f"xg_loaded{n}") for n in range(STEP)]
        y_stored = [sem(f"y_stored{n}") for n in range(STEP)]
        (idy_ready, xg_T, xgT_ready, up_mm, h_ready, down_mm, y_ready, summed) = map(sem, (
            "idy_ready", "xg_T", "xgT_ready", "up_mm", "h_ready", "down_mm", "y_ready", "summed"))
        yk_loaded = [sem(f"yk_loaded{n}") for n in range(4)]
        out_stored = [sem(f"out_stored{n}") for n in range(4)]

        def wait(eng, s, value):
            if not isinstance(value, int) or value > 0:
                eng.wait_ge(s, value)

        def wait_apart(eng, s, value):
            wait(eng, s, value)
            if not isinstance(value, int):
                eng.sem_inc(passed, 1)

        class Chain:

            def __init__(self, eng, s):
                self.eng, self.s, self.base, self.n = eng, s, 0, 0

            def link(self, ins):
                self.n += 1
                ins.then_inc(self.s, 1)
                wait_apart(self.eng, self.s, self.base + self.n)

            def enter(self, step, per):
                self.start, self.per = self.base + self.n, per
                self.base, self.n = step * per + self.start, 0

            def leave(self, steps):
                assert self.n == self.per
                self.base, self.n = self.start + steps * self.per, 0

        def key_tiles(b):
            return 4 * (b + 1)

        def tiles_before(b, g):
            return g * key_tiles(b) + 8 * b * (b + 1)

        def maxes_before(b, g):
            return g * (16 * (b + 1)) + 32 * b * (b + 1)

        def max_chunks(b):
            return [(tt, c, j) for tt in range(4) for c in range(b + 1) for j in range(J)]

        def bodies(eng, body):
            for g in range(2):
                body(0, g, 0, g + 2)
            for b in range(NB):
                if b:
                    with eng.Fori(0, 2) as g:
                        body(b, g, b, g + 2)
                if b + 1 < NB:
                    with eng.Fori(0, 2) as g:
                        body(b, g + 2, b + 1, g)
            for g in range(2):
                body(NB - 1, g + 2, None, g)

        def has_next(mb, mg):
            return mb is not None or mg == 0

        block = ctx.enter_context(nc.Block())

        @block.sync
        def _(sp):
            xt = x.rearrange("o (n p) h -> p (o n) h", p=P)
            xv = x_sb[:, :].rearrange("p (n h) -> p n h", h=H)
            sp.dma_start(xv[:, 0:4, :], xt[:, 0:4, :]).then_inc(ld_x[0], 16)
            sp.dma_start(c_sb[:, :], cst).then_inc(ld_c, 16)
            sp.dma_start(wqkv[:, :, :], w_qkv).then_inc(ld_qkv, 16)
            for n in range(1, 4):
                sp.dma_start(xv[:, 4 * n:4 * n + 4, :], xt[:, 4 * n:4 * n + 4, :]).then_inc(ld_x[n], 16)
            sp.dma_start(bq[:, :], b_q).then_inc(ld_w, 16)
            sp.dma_start(bk[:, :], b_k).then_inc(ld_w, 16)
            sp.dma_start(bv[:, :], b_v).then_inc(ld_w, 16)
            sp.dma_start(bo[:, :], b_o).then_inc(ld_w, 16)
            sp.dma_start(o_nrm[:, 0:2 * T], trig).then_inc(ld_w, 16)
            sp.dma_start(wo[:, :, :], w_o).then_inc(ld_late, 16)
            sp.dma_start(gate_sb[:, :, :], gate).then_inc(ld_late, 16)
            sp.dma_start(sh1[:, :, :], w_sh1).then_inc(ld_late, 16)
            sp.dma_start(sh2[:, :, :], w_sh2).then_inc(ld_late, 16)
            sp.wait_ge(q_zeroed, 1)
            sp.wait_ge(k_ones, 1)
            sp.sem_inc(qk_placed, 32 * J)
            with sp.Fori(0, NB) as b:
                sp.wait_ge(rot_done, b * 4 + 8)
                sp.dma_start(q_d[ds(b, 1)].rearrange("b j g (i a) t -> (b j g i) a t", a=2),
                             rot[:, 0:2, ds(b * QB, QB)]).then_inc(rot_stored, 16)
                sp.dma_start(k_d[ds(b, 1)].rearrange("b g (i a) t -> (b g i) a t", a=2),
                             rot[0:32, 2:4, ds(b * QB, QB)]).then_inc(rot_stored, 16)
                sp.wait_ge(rot_stored, b * 32 + 32)
                sp.wait_ge(qk_placed, b * (32 * J) + 32 * J)
                for j in range(J):
                    rows = slice(32 * j + MROWS, 32 * j + MROWS + HD)
                    sp.dma_start(q_aug[rows, ds(b * NKV, NKV), :],
                                 q_d[ds(b, 1), j].rearrange("b g r t -> (b r) g t")).then_inc(qk_placed, 16)
                    sp.dma_start(k_pad[rows, j, :].rearrange("p (g t) -> p g t", g=NKV)[:, :, ds(b * QB, QB)],
                                 k_d[ds(b, 1)].rearrange("b g r t -> (b r) g t")).then_inc(qk_placed, 16)

            def place_max_rows(u):
                wait_apart(sp, mT_copied, u + 1)
                for j in range(J):
                    rows = slice(32 * j, 32 * j + MROWS)
                    sp.dma_start(q_aug[rows, ds(u, 1), :], m_T[rows, :].unsqueeze(1)).then_inc(mrow_placed, 16)

            def move_sums(u):
                wait_apart(sp, pv_copied, u + 1)
                wait(sp, inverted, u)
                for j in range(J):
                    sp.dma_start(sums[32 * j:32 * j + 32, :],
                                 heads[32 * j + HD:32 * j + HD + 1, :].rearrange("p (r c) -> p r c", c=16)).then_inc(sums_moved, 16)
                wait_apart(sp, inverted, u + 1)
                wait(sp, scale_ready, u)
                for j in range(J):
                    sp.dma_start(scale_row[32 * j:32 * j + 1, :].rearrange("p (r c) -> p r c", c=16),
                                 inv_sums[32 * j:32 * j + 32, :]).then_inc(inv_moved, 16)

            def body(b, g, mb, mg):
                if not (isinstance(g, int) and b + g == 0):
                    move_sums(g + (4 * b - 1))
                if has_next(mb, mg):
                    place_max_rows(g + (4 * b + 1))

            place_max_rows(0)
            sp.wait_ge(scale_row_set, 1)
            bodies(sp, body)
            move_sums(UNITS - 1)

            sp.wait_ge(eob_ready, 1)

            def load_weights(it, s):
                expert = sp.value_load(eob[0:1, ds(it * STEP + s, 1)], min_val=0, max_val=E - 1)
                sp.wait_ge(down_mm, it * STEP + (s + 1))
                sp.dma_start(w1s[s % 4].unsqueeze(1), w1[:, ds(expert, 1), :, :]).then_inc(w_loaded[s % 4], 16)
                sp.dma_start(w2s[s % 4].unsqueeze(1), w2[:, ds(expert, 1), :, :]).then_inc(w_loaded[s % 4], 16)

            with sp.Fori(0, NBLK // STEP) as it:
                for s in range(STEP):
                    load_weights(it, s)
            for s in range(STEP):
                sp.wait_ge(y_stored[s], 16 * (NBLK // STEP))
            y_t = y_d.rearrange("(n p k) h -> p n (k h)", p=P, k=K)
            with sp.Fori(0, NT // 4) as it:
                for h in range(4):
                    sp.wait_ge(summed, it * 4 + (h + 1))
                    sp.dma_start(yk[h].unsqueeze(1), y_t[:, ds(it * 4 + h, 1), :]).then_inc(yk_loaded[h], 16)

        @block.gpsimd
        def _(gp):
            chain = Chain(gp, pool)
            nc.gpsimd.memset(v_all[:, :], 16.0).then_inc(v_ones, 1)
            chain.link(nc.gpsimd.memset(m_stage[:, :, :], 0.0))
            for j in range(J):
                gp.wait_ge(k_zeroed, j + 1)
                chain.link(nc.gpsimd.memset(k_pad[32 * j:32 * j + MROWS, j, :], 1.0))
            gp.sem_inc(k_ones, 1)

            gp.sem_inc(rot_done, 4)
            with gp.Fori(0, NB) as b:
                for n, op in enumerate((ALU.subtract, ALU.add, ALU.subtract, ALU.add)):
                    rows = P if n < 2 else 32
                    gp.wait_ge(rot_terms, b * 8 + (2 * n + 2))
                    nc.gpsimd.tensor_tensor(rot[0:rows, n, ds(b * QB, QB)], p_ring[0:rows, 2 * n, :],
                                            p_ring[0:rows, 2 * n + 1, :], op).then_inc(rot_done, 1)

            def stage_v(b, g):
                nst, before = key_tiles(b), tiles_before(b, g)
                for st in range(nst):
                    wait_apart(gp, pv_done, before + (4 - nst + st + 1) if st < nst - 4 else before)
                    nc.gpsimd.tensor_copy(v_cur[:, st, :], v_all[:, ds(g * (NT * 32) + st * 32, 32)]).then_inc(v_staged, 1)

            def split(u):
                part = [m_stage[:, :, :].rearrange("p t (j r) -> p t j r", j=J)[:, :, :, r] for r in range(MROWS)]
                neg, r1, r2 = (t[:, :].rearrange("p (t j) -> p t j", t=4) for t in (m_neg, m_r1, m_r2))
                gp.wait_ge(max_ready, u + 1)
                wait_apart(gp, mT_ready, u)
                chain.link(nc.gpsimd.tensor_scalar(m_neg[:, :], m_row[:, :], -1.0, None, ALU.mult))
                chain.link(nc.gpsimd.tensor_copy(part[0], neg))
                chain.link(nc.gpsimd.tensor_tensor(r1, neg, part[0], ALU.subtract))
                chain.link(nc.gpsimd.tensor_copy(part[1], r1))
                chain.link(nc.gpsimd.tensor_tensor(r2, r1, part[1], ALU.subtract))
                nc.gpsimd.tensor_copy(part[2], r2).then_inc(split_done, 1)

            def normalise(u):
                gp.wait_ge(scale_ready, u + 1)
                nc.gpsimd.tensor_tensor(o_nrm[:, ds(u * QB, QB)], heads, scale, ALU.mult).then_inc(o_done, 1)

            def body(b, g, mb, mg):
                stage_v(b, g)
                if has_next(mb, mg):
                    chain.base, chain.n = g * 5 + (split_links + 5 * (4 * b + 1)), 0
                    split(g + (4 * b + 1))
                if not (isinstance(g, int) and b + g == 0):
                    normalise(g + (4 * b - 1))

            gp.wait_ge(v_done, NB + 1)
            gp.wait_ge(xn_ready, NT)
            gp.wait_ge(ld_w, 16 * 5)
            for n in range(NT):
                nc.gpsimd.tensor_tensor(x_sb[:, n * H:(n + 1) * H], x_sb[:, n * H:(n + 1) * H], bo[:, :], ALU.add
                                        ).then_inc(xb_done, 1)
            split_links = chain.n
            split(0)
            bodies(gp, body)
            normalise(UNITS - 1)
            chain.base, chain.n = split_links + 5 * UNITS, 0

            gp.wait_ge(pv_done, tiles_before(NB - 1, NKV))
            nc.gpsimd.memset(ones_row, 1.0)
            nc.gpsimd.iota(row_i.rearrange("p (n k) -> p n k", k=K), [[P * K, NT], [1, K]], base=0, channel_multiplier=K
                           ).then_inc(late_consts, 1)
            gp.wait_ge(late_consts, 1)
            nc.gpsimd.tensor_copy(row_f, row_i).then_inc(late_consts, 1)
            gp.wait_ge(filled, 16 * UNITS)
            gp.wait_ge(slot_ready, 1)
            for n in range(NT):
                gp.wait_ge(staged, n + 1)
                for k in range(K):
                    at = n * K + k
                    gp.indirect_dma_start(
                        out=xs_d[:, :], out_offset=bass.IndirectOffsetOnAxis(ap=slot_i.bitcast(u32)[:, at:at + 1], axis=0),
                        in_=stage[n % 2][:, k, :], in_offset=None).then_inc(scattered[n % 2], 16)

            def scatter(it, s):
                gp.wait_ge(idy_ready, it * STEP + (s + 1 + STEP))
                wait_apart(gp, y_ready, it * STEP + (s + 3))
                gp.indirect_dma_start(
                    out=y_d[:, :], out_offset=bass.IndirectOffsetOnAxis(ap=ids_y[s].bitcast(u32), axis=0),
                    in_=ys[s], in_offset=None, bounds_check=ROWS - 1, oob_is_err=False).then_inc(y_stored[s], 16)

            with gp.Fori(0, NBLK // STEP) as it:
                for s in range(STEP):
                    scatter(it, s)

        @block.scalar
        def _(act):
            act.wait_ge(zero_set, 1)
            for j in range(J):
                nc.scalar.copy(k_pad[:, j, :].bitcast(f32), zero[:, :].to_broadcast([P, NKV * T // 2])).then_inc(k_zeroed, 1)
            act.sem_inc(xnT_ready, 2)
            with act.Fori(0, NB) as b:
                act.wait_ge(xn_used, b * 4 + 8)
                act.wait_ge(v_mm, b + 1)
                for c in range(CH):
                    nc.scalar.copy(xnT[:, c, :], bank[c][:, :]).then_inc(xnT_ready, 1)

            def copy_max_rows(u):
                act.wait_ge(mT_ready, u + 1)
                wait(act, mrow_placed, u * (16 * J))
                nc.scalar.copy(m_T[:, :], bank16[7][:, 0:QB]).then_inc(mT_copied, 1)

            xs_fill = xs_d.rearrange("(b p) w -> p b w", p=P)
            act.wait_ge(fill_set, 1)
            act.wait_ge(rot_done, NB * 4 + 4)

            def body(b, g, mb, mg):
                before = tiles_before(b, g)
                act.dma_start(xs_fill[:, ds((g + 4 * b) * (NBLK // UNITS), NBLK // UNITS), :],
                              fill.unsqueeze(1).to_broadcast([P, NBLK // UNITS, RW])).then_inc(filled, 16)
                for st in range(key_tiles(b)):
                    if st == key_tiles(b) - 1 and has_next(mb, mg):
                        copy_max_rows(g + (4 * b + 1))
                    at = 128 * max(0, st - 4 * b)
                    for j in range(J):
                        chunk = 4 * st + j
                        act.wait_ge(sk_ready, before * 4 + (chunk + 1))
                        if j == 0:
                            wait(act, pv_done, before + (st - 1))
                        nc.scalar.activation(p_ring[:, chunk % 8, at:QB], S_K[j % 2][:, at:QB], ACT.Exp).then_inc(p_ready, 1)
                act.wait_ge(pv_done, before + key_tiles(b))
                wait(act, o_done, g + 4 * b)
                nc.scalar.copy(heads, PV[:, :]).then_inc(pv_copied, 1)

            copy_max_rows(0)
            bodies(act, body)

            for b in range(NB):
                act.wait_ge(xn2_used, b + 1)
                for c in range(CH):
                    nc.scalar.copy(xn2T[:, c, b * QB:(b + 1) * QB], bank[2 + 2 * (b % 2) + c][:, :]).then_inc(xn2T_ready, 1)
            for h in range(2):
                act.wait_ge(logit_sub, h + 1)
                nc.scalar.activation(ex[h], lg[h], ACT.Exp).then_inc(exp_done, 1)
            act.wait_ge(hot_mm, 1)
            for n in range(2):
                last = nc.scalar.copy(hotT[:, n * 1024:(n + 1) * 1024], bank16[6 + n][0:E, :])
            last.then_inc(hotT_done, 1)

            def stage_tile(b, m):
                if isinstance(b, int):
                    wait(act, scattered[m % 2], m // 2 * (16 * K))
                else:
                    act.wait_ge(scattered[m % 2], b * (32 * K) + m // 2 * (16 * K))
                nc.scalar.copy(stage[m % 2][:, :, 0:H], xn2_all[:, ds(b * (4 * H) + m * H, H)].unsqueeze(1).to_broadcast([P, K, H]))
                nc.scalar.copy(stage[m % 2][:, :, H], row_f[:, ds(b * (4 * K) + m * K, K)]).then_inc(staged, 1)

            act.wait_ge(slot_ready, 1)
            act.wait_ge(xn2_ready, NT)
            act.wait_ge(late_consts, 2)

            def gates_and_tiles(b):
                for m in range(4):
                    act.wait_ge(sh_mm, b * 4 + (m + 1))
                    act.wait_ge(hs_ready, b * 4 + (m + 1))
                    nc.scalar.activation(sg[:, m % 2, :], bank[m % 2][0:HI, :], ACT.Silu).then_inc(sg_ready, 1)
                    stage_tile(b, m)

            gates_and_tiles(0)
            with act.Fori(1, NB) as b:
                gates_and_tiles(b)

            xs_v = xs_d.rearrange("(b p) w -> p b w", p=P)
            for h in range(2):
                act.wait_ge(scattered[h], 16 * NT * K // 2)

            def load_rows(it, s):
                act.wait_ge(idy_ready, it * STEP + (s + 1))
                act.dma_start(xg[s].unsqueeze(1), xs_v[:, ds(it * STEP + s, 1), :]).then_inc(xg_loaded[s], 16)

            def silu(it, s):
                act.wait_ge(up_mm, it * STEP + (s + 3))
                act.wait_ge(down_mm, it * STEP + (s + 3))
                nc.scalar.activation(hT[s % 2], bank[2 + s % 2][0:HI, 0:2 * P], ACT.Silu).then_inc(h_ready, 1)

            def copy_y(it, s):
                act.wait_ge(down_mm, it * STEP + (s + 5))
                wait(act, y_stored[s], it * 16)
                nc.scalar.copy(ys[s], bank[4 + s % 2][:, 0:H]).then_inc(y_ready, 1)

            act.sem_inc(h_ready, 2)
            act.sem_inc(y_ready, 2)
            for s in range(6):
                load_rows(0, s)
            silu(0, 0)

            def silu_and_copy(it):
                for s in range(STEP):
                    silu(it + (s + 1) // STEP, (s + 1) % STEP)
                    load_rows(it + (s + 6) // STEP, (s + 6) % STEP)
                    copy_y(it, s)

            silu_and_copy(0)
            with act.Fori(1, NBLK // STEP - 1) as it:
                silu_and_copy(it)
            for s in range(STEP):
                if s < STEP - 1:
                    silu(NBLK // STEP - 1, s + 1)
                if s < STEP - 6:
                    load_rows(NBLK // STEP - 1, s + 6)
                copy_y(NBLK // STEP - 1, s)
            for h in range(4):
                act.sem_inc(out_stored[h], 16)
            out_t = out.rearrange("o (n p) h -> p (o n) h", p=P)
            with act.Fori(0, NT // 4) as it:
                for h in range(4):
                    act.wait_ge(summed, it * 4 + (h + 5))
                    act.dma_start(out_t[:, ds(it * 4 + h, 1), :], acc[h].unsqueeze(1)).then_inc(out_stored[h], 16)
            for h in range(4):
                act.wait_ge(out_stored[h], 16 * (NT // 4) + 16)

        @block.vector
        def _(v):
            chain = Chain(v, dve)
            link = chain.link
            nc.vector.memset(zero[:, :], 0.0).then_inc(zero_set, 1)
            nc.vector.memset(q_aug[:, :, :].rearrange("p a b -> p (a b)").bitcast(f32), 0.0).then_inc(q_zeroed, 1)
            v.wait_ge(ld_c, 16)
            nc.vector.tensor_copy(ident16[:, :], ident)
            nc.vector.tensor_copy(kmask16[:, :], kmask).then_inc(consts16, 1)

            def inv_sqrt(n, at=0):
                var, y, y2, half = mv_all[:, at:at + n, 1], rstd[:, at:at + n], rs_tmp[:, 0, 0:n], rs_tmp[:, 1, 0:n]
                link(nc.vector.tensor_scalar(half, var, EPS, None, ALU.add))
                link(nc.vector.tensor_scalar(y2.bitcast(i32), half.bitcast(i32), 1, None, ALU.logical_shift_right))
                nc.vector.tensor_scalar(half, half, 0.5, None, ALU.mult)
                link(nc.vector.tensor_scalar(y.bitcast(i32), y2.bitcast(i32), -1.0, float(0x5F3759DF), ALU.mult, ALU.add))
                for _ in range(3):
                    link(nc.vector.scalar_tensor_tensor(y2, y, -1.0, y, ALU.mult, ALU.mult))
                    link(nc.vector.tensor_tensor(y2, y2, half, ALU.mult))
                    link(nc.vector.scalar_tensor_tensor(y, y2, 1.5, y, ALU.add, ALU.mult))

            mv_all = mv[:, :].rearrange("p (n w) -> p n w", w=2)

            def statistics(tiles):
                for n in tiles:
                    if n % 4 == 0:
                        v.wait_ge(ld_x[n // 4], 16)
                    last = nc.vector.bn_stats(stats[:, n, :], x_sb[:, n * H:(n + 1) * H])
                link(last)
                for n in tiles:
                    last = nc.vector.bn_aggr(mv[:, 2 * n:2 * n + 2], stats[:, n, :])
                link(last)
                inv_sqrt(len(tiles), tiles[0])

            def normalise_rows(b, used):
                wait(v, xn_used, used)
                for tt in range(4):
                    nc.vector.tensor_scalar(xn[:, tt, :], x_sb[:, ds(b * (4 * H) + tt * H, H)], mv[:, ds(b * 8 + 2 * tt, 1)],
                                            rstd[:, ds(b * 4 + tt, 1)], ALU.subtract, ALU.mult).then_inc(xn_ready, 1)

            v_rows = v_all[:, :].rearrange("p (g m) -> p g m", g=NKV)

            def biases_and_rotation(b):
                for part, (mm, bias, rows) in enumerate(((q_mm, bq, P), (k_mm, bk, 32))):
                    even, odd = bank[2 + 2 * part][0:rows, :], bank[3 + 2 * part][0:rows, :]
                    v.wait_ge(rot_done, b * 4 + (2 * part + 2))
                    v.wait_ge(mm, b + 1)
                    for n, (src, w, tabl) in enumerate(((even, 0, cos), (odd, 1, sin), (even, 0, sin), (odd, 1, cos))):
                        nc.vector.scalar_tensor_tensor(p_ring[0:rows, 4 * part + n, :], src, bias[0:rows, w:w + 1],
                                                       tabl[0:rows, ds(b * QB, QB)], ALU.add, ALU.mult).then_inc(rot_terms, 1)
                v.wait_ge(v_mm, b + 2)
                v_ps = bank[6][:, 0:4 * NKV * HD].rearrange("p (n g d) -> p n g d", n=4, g=NKV)
                bv_g = bv[:, :].rearrange("p (g d) -> p g d", g=NKV)
                for tt in range(4):
                    last = nc.vector.tensor_tensor(v_rows[:, :, ds(b * 128 + tt * 32, HD)], v_ps[:, tt, :, :], bv_g, ALU.add)
                last.then_inc(v_done, 1)

            statistics(range(4))
            normalise_rows(0, 0)
            statistics(range(4, NT))
            v.wait_ge(ld_w, 16 * 5)
            v.wait_ge(v_ones, 1)
            v.sem_inc(v_done, 1)
            with v.Fori(0, NB - 1) as b:
                normalise_rows(b + 1, b * 4 + 8)
                biases_and_rotation(b)
            biases_and_rotation(NB - 1)

            nc.vector.memset(scale_row, 1.0).then_inc(scale_row_set, 1)
            v.wait_ge(xn_used, NT + 4)
            nc.vector.memset(fill, float(ROWS)).then_inc(fill_set, 1)

            def row_max(b, g, n):
                tt, c, j = max_chunks(b)[n]
                src = S_Q[n % 4]
                at = m_part[:, tt * J + j, c:c + 1]
                (v.wait_ge if c < b else lambda *a: wait_apart(v, *a))(sq_ready, maxes_before(b, g) + (n + 1))
                if c < b:
                    nc.vector.reduce_max(at, src[:, :], AX.X).then_inc(sq_used, 1)
                else:
                    w = 128 * (tt + 1)
                    nc.vector.tensor_tensor_reduce(out=src[:, 0:w], in0=src[:, 0:w], in1=qmask[:, 512 - w:512], scale=1.0,
                                                   scalar=-3.0e38, op0=ALU.add, op1=ALU.max, accum_out=at).then_inc(sq_used, 1)

            def row_max_all(b, g, u, between=None):
                wait_apart(v, max_ready, u)
                for n in range(16 * (b + 1)):
                    row_max(b, g, n)
                    if between:
                        between(n + 1)
                v.wait_ge(sq_used, maxes_before(b, g) + 16 * (b + 1))
                wait(v, split_done, u)
                nc.vector.reduce_max(m_row[:, :], m_part[:, :, 0:b + 1], AX.X).then_inc(max_ready, 1)

            def invert_sums(u):
                v.wait_ge(sums_moved, (u + 1) * (16 * J))
                nc.vector.reciprocal(inv_sums[:, :], sums[:, :]).then_inc(inverted, 1)

            def spread_scale(u):
                v.wait_ge(inv_moved, (u + 1) * (16 * J))
                wait_apart(v, o_done, u)
                nc.vector.stream_shuffle(scale, scale_row, [0] * 32).then_inc(scale_ready, 1)

            def body(b, g, mb, mg):
                def between(n):
                    if n == 8:
                        invert_sums(g + (4 * b - 1))
                    if n == 16:
                        spread_scale(g + (4 * b - 1))

                if isinstance(g, int) and b + g == 0:
                    between = None
                if mb is not None:
                    row_max_all(mb, mg, g + (4 * b + 2), between)
                else:
                    between(8)
                    between(16)

            row_max_all(0, 0, 0)
            row_max_all(0, 1, 1)
            bodies(v, body)
            invert_sums(UNITS - 1)
            spread_scale(UNITS - 1)

            v.wait_ge(xb_done, NT)
            for h in range(2):
                tiles = range(8 * h, 8 * h + 8)
                for n in tiles:
                    xs = x_sb[:, n * H:(n + 1) * H]
                    v.wait_ge(wo_mm, n + 1)
                    nc.vector.tensor_tensor(xs, bank[n % 2][:, 0:H], xs, ALU.add).then_inc(x1_done, 1)
                v.wait_ge(x1_done, 8 * h + 8)
                for n in tiles:
                    last = nc.vector.bn_stats(stats[:, n, :], x_sb[:, n * H:(n + 1) * H])
                link(last)
                for n in tiles:
                    last = nc.vector.bn_aggr(mv[:, 2 * n:2 * n + 2], stats[:, n, :])
                link(last)
                inv_sqrt(8, 8 * h)
                for n in tiles:
                    nc.vector.tensor_scalar(xn2_all[:, n * H:(n + 1) * H], x_sb[:, n * H:(n + 1) * H], mv[:, 2 * n:2 * n + 1],
                                            rstd[:, n:n + 1], ALU.subtract, ALU.mult).then_inc(xn2_ready, 1)
            def each(t):
                return t.rearrange("p (n e) -> p n e", n=8)

            v.wait_ge(filled, 16 * UNITS)
            for h in range(2):
                v.wait_ge(logit_mm, h + 1)
                logits = each(bank[6 + h][:, :])
                link(nc.vector.reduce_max(row8[h], logits, AX.X))
                nc.vector.tensor_tensor(each(lg[h]), logits, row8[h].unsqueeze(2).to_broadcast([P, 8, E]), ALU.subtract
                                        ).then_inc(logit_sub, 1)
            for h in range(2):
                v.wait_ge(exp_done, h + 1)
                link(nc.vector.reduce_sum(sum8, each(ex[h]), AX.X))
                link(nc.vector.reciprocal(sum8, sum8))
                link(nc.vector.tensor_tensor(each(pr), each(ex[h]), sum8.unsqueeze(2).to_broadcast([P, 8, E]), ALU.mult))
                for t in range(8):
                    last = nc.vector.max(top8[:, 8 * t:8 * t + 8], pr[:, E * t:E * t + E])
                link(last)
                for t in range(8):
                    last = nc.vector.max_index(idx8[:, 8 * t:8 * t + 8], top8[:, 8 * t:8 * t + 8], pr[:, E * t:E * t + E])
                link(last)
                link(nc.vector.reduce_sum(sum6, each(top8)[:, :, 0:K], AX.X))
                link(nc.vector.reciprocal(sum6, sum6))
                link(nc.vector.tensor_tensor(each(wts[:, h * 8 * K:(h + 1) * 8 * K]), each(top8)[:, :, 0:K],
                                             sum6.unsqueeze(2).to_broadcast([P, 8, K]), ALU.mult))
                link(nc.vector.tensor_copy(idxf, idx8))
                hot_h = hot[:, h * 8 * K * E:(h + 1) * 8 * K * E]
                for t in range(8):
                    last = nc.vector.tensor_tensor(
                        hot_h[:, t * K * E:(t + 1) * K * E].rearrange("p (k e) -> p k e", k=K),
                        iota_e.unsqueeze(1).to_broadcast([P, K, E]),
                        idxf[:, 8 * t:8 * t + K].unsqueeze(2).to_broadcast([P, K, E]), ALU.is_equal)
                link(last)
                with nc.allow_low_precision("sums of six zeros and ones"):
                    nc.vector.reduce_sum(each(chosen[:, h * 8 * E:(h + 1) * 8 * E]),
                                         hot_h.rearrange("p (n k e) -> p n e k", n=8, k=K), AX.X).then_inc(chosen_ready, 1)

            v.wait_ge(hotT_done, 1)
            v.wait_ge(late_consts, 2)
            link(nc.vector.tensor_tensor_scan(cum, ones_row, hotT, 0.0, ALU.mult, ALU.add))
            c_int = cnt.bitcast(i32)
            link(nc.vector.tensor_scalar(c_int[:, 0:1], cum[:, T - 1:T], float(P - 1), None, ALU.add))
            link(nc.vector.tensor_scalar(c_int[:, 1:2], c_int[:, 0:1], -P, None, ALU.bitwise_and))
            nc.vector.tensor_copy(cnt[:, 2:3], c_int[:, 1:2]).then_inc(padded, 1)
            v.wait_ge(base_mm, 1)
            nc.vector.tensor_copy(cnt[:, 4:5], bank[5][0:E, 1:2])
            link(nc.vector.tensor_scalar(cnt[:, 3:4], bank[5][0:E, 0:1], -1.0, None, ALU.add))
            nc.vector.tensor_scalar(past_end, blk_start, cnt[:, 4:5], None, ALU.is_ge).then_inc(past_ready, 1)
            nc.vector.tensor_scalar(cum, cum, cnt[:, 3:4], None, ALU.add).then_inc(slotT_ready, 1)
            for n in range(2):
                v.wait_ge(slotT_mm, n + 1)
                hv = hot[:, n * 8 * K * E:(n + 1) * 8 * K * E].rearrange("p (n k e) -> p n k e", n=8, k=K)
                sv = bank[6 + n][:, :].rearrange("p (n e) -> p n e", n=8)
                for t in range(8):
                    last = nc.vector.tensor_tensor(prod.rearrange("p (n k e) -> p n k e", n=8, k=K)[:, t, :, :], hv[:, t, :, :],
                                                   sv[:, t, :].unsqueeze(1).to_broadcast([P, K, E]), ALU.mult)
                link(last)
                link(nc.vector.reduce_sum(slot[:, n * 8 * K:(n + 1) * 8 * K].rearrange("p (n k) -> p n k", k=K),
                                          prod.rearrange("p (n k e) -> p n k e", n=8, k=K), AX.X))
            nc.vector.tensor_copy(slot_i, slot).then_inc(slot_ready, 1)
            v.wait_ge(eob_mm, 1)
            link(nc.vector.tensor_scalar(past_end[0:1, :], bank[5][0:1, 2:2 + NBLK], float(E - 1), None, ALU.min))
            nc.vector.tensor_copy(eob, past_end[0:1, :]).then_inc(eob_ready, 1)

            v.sem_inc(hs_ready, 2)
            v.sem_inc(sh_added, 2)
            with v.Fori(0, NB) as b:
                v.wait_ge(shd_mm, b * 4 + 4)
                for m in range(4):
                    v.wait_ge(sg_ready, b * 4 + (m + 1))
                    nc.vector.tensor_tensor(hs[:, m, :], bank[2 + m % 2][0:HI, :], sg[:, m % 2, :], ALU.mult).then_inc(hs_ready, 1)
                for tt in range(4):
                    xs = x_sb[:, ds(b * (4 * H) + tt * H, H)]
                    v.wait_ge(shd_mm, b * 4 + (tt + 5))
                    nc.vector.tensor_tensor(xs, bank[4 + tt % 2][:, 0:H], xs, ALU.add).then_inc(sh_added, 1)

            def rows_T(it, s):
                v.wait_ge(xg_T, it * STEP + (s + 5))
                v.wait_ge(up_mm, it * STEP + (s + 1))
                nc.vector.tensor_copy(xgT[s % 2], bank[s % 2][:, 0:H]).then_inc(xgT_ready, 1)
                wait(v, y_stored[s], it * 16)
                nc.vector.tensor_copy(ids_y[s], xg[s][:, H:RW]).then_inc(idy_ready, 1)

            v.sem_inc(xgT_ready, 2)
            v.sem_inc(idy_ready, STEP)

            def blocks(it):
                for s in range(STEP):
                    rows_T(it, s)

            blocks(0)
            with v.Fori(1, NBLK // STEP - 1) as it:
                blocks(it)
            for s in range(STEP):
                rows_T(NBLK // STEP - 1, s)

            v.sem_inc(summed, 4)
            with v.Fori(0, NT // 4) as it:
                chain.enter(it, 4 * (K - 1))
                for h in range(4):
                    v.wait_ge(yk_loaded[h], it * 16 + 16)
                    v.wait_ge(out_stored[h], it * 16 + 16)
                    for k in range(K):
                        prev = x_sb[:, ds(it * (4 * H) + h * H, H)] if k == 0 else acc[h]
                        ins = nc.vector.scalar_tensor_tensor(acc[h], yk[h][:, k * H:(k + 1) * H],
                                                             wts[:, ds(it * (4 * K) + (h * K + k), 1)], prev, ALU.mult, ALU.add)
                        if k < K - 1:
                            link(ins)
                        else:
                            ins.then_inc(summed, 1)
                chain.leave(NT // 4)

        @block.tensor
        def _(pe):
            def mm(o, lhsT, rhs, first=True, last=True):
                return nc.tensor.matmul(o, lhsT, rhs, start=first, stop=last)

            pe.wait_ge(ld_c, 16)
            pe.wait_ge(ld_qkv, 16)
            pe.sem_inc(xn_used, 4)
            pe.sem_inc(v_mm, 1)

            def rows_to_T(b):
                for tt in range(4):
                    pe.wait_ge(xn_ready, b * 4 + (tt + 1))
                    for c in range(CH):
                        last = nc.tensor.transpose(bank[c][:, tt * P:(tt + 1) * P], xn[:, tt, c * P:(c + 1) * P], ident)
                    last.then_inc(xn_used, 1)

            def qkv(b):
                pe.wait_ge(xnT_ready, b * 2 + 4)
                cols = ((2, 0, P, q_mm), (3, P, P, q_mm), (4, 2 * P, 32, k_mm), (5, 2 * P + 32, 32, k_mm))
                for n, (bk_n, at, m, done) in enumerate(cols):
                    if n % 2 == 0:
                        wait(pe, rot_terms, b * 8 + (2 * n - 4))
                    for c in range(CH):
                        last = mm(bank[bk_n][0:m, :], wqkv[:, c, at:at + m], xnT[:, c, :], c == 0, c == CH - 1)
                    if n % 2:
                        last.then_inc(done, 1)
                pe.wait_ge(v_done, b + 1)
                for tt in range(4):
                    for c in range(CH):
                        last = mm(bank[6][:, tt * 64:(tt + 1) * 64], xnT[:, c, tt * P:(tt + 1) * P],
                                  wqkv[:, c, 320:384], c == 0, c == CH - 1)
                last.then_inc(v_mm, 1)

            rows_to_T(0)
            qkv(0)
            rows_to_T(1)
            with pe.Fori(1, NB - 1) as b:
                qkv(b)
                rows_to_T(b + 1)
            qkv(NB - 1)

            def score_q(b, g, n):
                tt, c, j = max_chunks(b)[n]
                w = QB if c < b else 128 * (tt + 1)
                before = maxes_before(b, g)
                wait(pe, sq_used, before + (n - 3))
                mm(S_Q[n % 4][:, 0:w], q_aug[:, ds(g + 4 * b, 1), tt * P:(tt + 1) * P].rearrange("p u t -> p (u t)"),
                   k_pad[:, j, ds(g * T + c * QB, w)]).then_inc(sq_ready, 1)

            def score_k(b, g, st, j):
                n, before = 4 * st + j, tiles_before(b, g)
                at = 128 * max(0, st - 4 * b)
                diagonal = st >= 4 * b
                wait(pe, p_ready, before * 4 + (n - 1))
                o = S_K[j % 2]
                last = mm(o[:, at:QB], k_pad[:, j, ds(g * T + st * P, P)],
                          q_aug[:, ds(g + 4 * b, 1), at:QB].rearrange("p u t -> p (u t)"), True, not diagonal)
                if diagonal:
                    last = mm(o[:, at:at + P], ident16[:, :], kmask16[:, :], False, True)
                last.then_inc(sk_ready, 1)

            def p_times_v(b, g, st):
                before = tiles_before(b, g)
                at = 128 * max(0, st - 4 * b)
                pe.wait_ge(p_ready, before * 4 + (4 * st + 4))
                pe.wait_ge(v_staged, before + (st + 1))
                if st == 0:
                    wait(pe, pv_copied, g + 4 * b)
                for j in range(J):
                    last = mm(PV[32 * j:32 * j + 32, at:QB], v_cur[:, st, :], p_ring[:, (4 * st + j) % 8, at:QB],
                              st == 0, st == key_tiles(b) - 1)
                last.then_inc(pv_done, 1)

            def transpose_max(u):
                pe.wait_ge(split_done, u + 1)
                wait(pe, mT_copied, u)
                for tt in range(4):
                    last = nc.tensor.transpose(bank16[7][:, tt * P:(tt + 1) * P], m_stage[:, tt, :], ident16[:, :])
                last.then_inc(mT_ready, 1)

            def body(b, g, mb, mg):
                nst = key_tiles(b)
                n_max = 16 * (mb + 1) if mb is not None else 0
                if mb is not None:
                    pe.wait_ge(qk_placed, 32 * J * (mb + 2))
                pe.wait_ge(mrow_placed, g * (16 * J) + (4 * b + 1) * 16 * J)
                for st in range(nst):
                    if st == nst - 2 and has_next(mb, mg):
                        transpose_max(g + (4 * b + 1))
                    todo = list(range(n_max * st // nst, n_max * (st + 1) // nst))
                    for j in range(J):
                        for n in todo[len(todo) * j // J:len(todo) * (j + 1) // J]:
                            score_q(mb, mg, n)
                        score_k(b, g, st, j)
                    if st:
                        p_times_v(b, g, st - 1)
                p_times_v(b, g, nst - 1)

            pe.wait_ge(consts16, 1)
            pe.wait_ge(v_done, NB + 1)
            pe.wait_ge(qk_placed, 32 * J * 2)
            for g in range(2):
                for n in range(16):
                    score_q(0, g, n)
            transpose_max(0)
            bodies(pe, body)

            pe.wait_ge(ld_late, 16 * 4)
            pe.wait_ge(o_done, UNITS)
            for n in range(NT):
                wait(pe, x1_done, n - 1)
                for g in range(NKV):
                    at = (n // 4 * NKV + g) * QB + n % 4 * P
                    last = mm(bank[n % 2][:, 0:H], o_nrm[:, at:at + P], wo[:, g, :], g == 0, g == NKV - 1)
                last.then_inc(wo_mm, 1)

            def xn2_to_T(b):
                wait(pe, xn2T_ready, 2 * (b - 1))
                for n in range(4 * b, 4 * b + 4):
                    pe.wait_ge(xn2_ready, n + 1)
                    for c in range(CH):
                        last = nc.tensor.transpose(bank[2 + 2 * (b % 2) + c][:, n % 4 * P:(n % 4 + 1) * P],
                                                   xn2_all[:, n * H + c * P:n * H + (c + 1) * P], ident)
                last.then_inc(xn2_used, 1)

            xn2_to_T(0)
            for b in range(NB):
                if b + 1 < NB:
                    xn2_to_T(b + 1)
                pe.wait_ge(xn2T_ready, 2 * b + 2)
                for n in range(4 * b, 4 * b + 4):
                    for c in range(CH):
                        last = mm(bank[6 + n // 8][:, n % 8 * E:(n % 8 + 1) * E], xn2T[:, c, n * P:(n + 1) * P], gate_sb[:, c, :],
                                  c == 0, c == CH - 1)
                if b % 2:
                    last.then_inc(logit_mm, 1)

            pe.wait_ge(chosen_ready, 2)
            for n in range(NT):
                last = nc.tensor.transpose(bank16[6 + n // 8][0:E, n % 8 * P:(n % 8 + 1) * P], chosen[:, n * E:(n + 1) * E], ident16[:, :])
            last.then_inc(hot_mm, 1)
            pe.wait_ge(padded, 1)
            mm(bank[5][0:E, 0:1], tri_before, cnt[:, 2:3])
            mm(bank[5][0:E, 1:2], tri_upto, cnt[:, 2:3]).then_inc(base_mm, 1)
            pe.wait_ge(past_ready, 1)
            mm(bank[5][0:1, 2:2 + NBLK], ones_col, past_end).then_inc(eob_mm, 1)
            pe.wait_ge(slotT_ready, 1)
            for n in range(NT):
                last = nc.tensor.transpose(bank[6 + n // 8][:, n % 8 * E:(n % 8 + 1) * E], cum[:, n * P:(n + 1) * P], ident[0:E, 0:E])
                if n % 8 == 7:
                    last.then_inc(slotT_mm, 1)
            pe.wait_ge(eob_ready, 1)
            pe.sem_inc(shd_mm, 4)
            with pe.Fori(0, NB) as b:
                for m in range(4):
                    pe.wait_ge(hs_ready, b * 4 + (m + 1))
                    for half in range(2):
                        at = half * SI + m * HI
                        for c in range(CH):
                            last = mm(bank[2 * half + m % 2][0:HI, :], sh1[:, c, at:at + HI], xn2T[:, c, ds(b * QB, QB)],
                                      c == 0, c == CH - 1)
                    last.then_inc(sh_mm, 1)
                pe.wait_ge(hs_ready, b * 4 + 6)
                for tt in range(4):
                    pe.wait_ge(sh_added, b * 4 + (tt + 1))
                    for m in range(4):
                        last = mm(bank[4 + tt % 2][:, 0:H], hs[:, m, tt * P:(tt + 1) * P], sh2[:, m, :], m == 0, m == 3)
                    last.then_inc(shd_mm, 1)

            def rows_T(it, s):
                pe.wait_ge(xg_loaded[s], it * 16 + 16)
                pe.wait_ge(xgT_ready, it * STEP + (s + 1))
                for c in range(CH):
                    last = nc.tensor.transpose(bank[s % 2][:, c * P:(c + 1) * P], xg[s][:, c * P:(c + 1) * P], ident)
                last.then_inc(xg_T, 1)

            def up(it, s):
                pe.wait_ge(w_loaded[s % 4], it * (STEP // 4 * 32) + (s // 4 * 32 + 32))
                pe.wait_ge(xgT_ready, it * STEP + (s + 3))
                pe.wait_ge(h_ready, it * STEP + (s + 1))
                for i in range(2):
                    for c in range(CH):
                        last = mm(bank[2 + s % 2][0:HI, i * P:(i + 1) * P], w1s[s % 4][:, c, i * HI:(i + 1) * HI],
                                  xgT[s % 2][:, c * P:(c + 1) * P], c == 0, c == CH - 1)
                last.then_inc(up_mm, 1)

            def down(it, s):
                pe.wait_ge(h_ready, it * STEP + (s + 3))
                pe.wait_ge(y_ready, it * STEP + (s + 1))
                for i in range(2):
                    last = mm(bank[4 + s % 2][:, 0:H], hT[s % 2][:, i * P:(i + 1) * P], w2s[s % 4][:, i, :], i == 0, i == 1)
                last.then_inc(down_mm, 1)

            pe.wait_ge(sh_added, NT + 2)
            pe.sem_inc(xg_T, 4)
            pe.sem_inc(up_mm, 2)
            pe.sem_inc(down_mm, 4)
            rows_T(0, 0)
            rows_T(0, 1)
            up(0, 0)
            with pe.Fori(0, NBLK // STEP - 1) as it:
                for s in range(STEP):
                    rows_T(it + (s + 2) // STEP, (s + 2) % STEP)
                    up(it + (s + 1) // STEP, (s + 1) % STEP)
                    down(it, s)
            end = NBLK // STEP - 1
            for s in range(STEP):
                if s < STEP - 2:
                    rows_T(end, s + 2)
                if s < STEP - 1:
                    up(end, s + 1)
                down(end, s)


_INS = ["x", "w_qkv", "b_q", "b_k", "b_v", "b_o", "w_o", "gate", "w_sh1", "w_sh2", "w1", "w2", "trig", "cst"]


def constants():
    freqs = (np.float32(10000.0) ** -(np.arange(0, H, 2, dtype=np.float32) / np.float32(H)))[:HD // 2]
    ang = np.outer(freqs, np.arange(T, dtype=np.float32)).astype(np.float32)
    rows = np.tile(ang.astype(np.float64), (P // (HD // 2), 1))
    trig = np.concatenate([np.cos(rows), np.sin(rows)], axis=1).astype(np.float32)
    p, c = np.arange(P)[:, None], np.arange(512)[None, :]
    cst = np.zeros((P, 1121), np.float32)
    cst[:, 0:128] = np.eye(P)
    cst[:, 128:640] = np.where(c <= 384 + p, 0.0, BIG)
    cst[:, 640:768] = np.where(c[:, :P] >= p, 0.0, BIG)
    cst[:, 768:832] = np.arange(E)
    cst[:, 832:896] = p < c[:, :E]
    cst[:, 896:960] = p <= c[:, :E]
    cst[:, 960:1120] = np.arange(NBLK) * P
    cst[:, 1120] = 1.0
    return trig, cst


def laid_out(a):
    def chunks(w, rows):
        return w.reshape(-1, rows, w.shape[-1]).transpose(1, 0, 2)

    def q_cols(w):
        w = w.reshape(-1, NKV, J, HD // 2, 2).transpose(0, 2, 1, 3, 4)
        return [w[..., n].reshape(w.shape[0], -1) for n in range(2)]

    def k_cols(w):
        w = w.reshape(-1, NKV, HD // 2, 2)
        return [w[..., n].reshape(w.shape[0], -1) for n in range(2)]

    qe, qo = q_cols(a["L0_attn_Wq"])
    ke, ko = k_cols(a["L0_attn_Wk"])
    bqe, bqo = q_cols(a["L0_attn_bq"][None, :])
    bke, bko = k_cols(a["L0_attn_bk"][None, :])
    wo = np.zeros((J, 32, NKV, H), np.float32)
    wo[:, :HD] = a["L0_attn_Wo"].reshape(NKV, J, HD, H).transpose(1, 2, 0, 3)
    trig, cst = constants()
    return {
        "x": a["L0_attn_x"],
        "w_qkv": chunks(np.concatenate([qe, qo, ke, ko, a["L0_attn_Wv"]], axis=1), P),
        "b_q": np.stack([bqe[0], bqo[0]], axis=1),
        "b_k": np.stack([bke[0], bko[0]], axis=1),
        "b_v": np.broadcast_to(a["L0_attn_bv"], (P, NKV * HD)),
        "b_o": np.broadcast_to(a["L0_attn_bo"], (P, H)),
        "w_o": wo.reshape(P, NKV, H),
        "gate": chunks(a["L0_ffn_gate_w"].T, P),
        "w_sh1": chunks(a["L0_ffn_shared_gate_up"].T, P),
        "w_sh2": chunks(a["L0_ffn_shared_down"].T, HI),
        "w1": a["L0_ffn_experts_w1"].reshape(E, I, CH, P).transpose(3, 0, 2, 1),
        "w2": a["L0_ffn_experts_w2"].reshape(E, H, 2, HI).transpose(3, 0, 2, 1),
        "trig": trig,
        "cst": cst,
    }


def kernel(**inputs):
    import concourse.bacc as _bacc
    from concourse.bass_utils import run_bass_kernel_spmd as _run

    arrays = {f"in_{k}": np.ascontiguousarray(v) for k, v in laid_out({k: np.asarray(v) for k, v in inputs.items()}).items()}
    nc = _bacc.Bacc("TRN2", target_bir_lowering=False, num_devices=1)
    args = [nc.dram_tensor(f"in_{n}", arrays[f"in_{n}"].shape, mybir.dt.from_np(arrays[f"in_{n}"].dtype),
                           kind="ExternalInput").ap() for n in _INS]
    out = nc.dram_tensor("out", (1, T, H), mybir.dt.float32, kind="ExternalOutput").ap()
    preln_attention_moe(nc, *args, out)
    r = _run(nc, [arrays], core_ids=[0])
    return r.results[0]["out"]
```

```python
import concourse.bass as bass
from concourse import mybir
from contextlib import ExitStack
import numpy as np

T, H = 2048, 256
NH, NKV, HD = 16, 4, 16
E, I, K = 64, 176, 6
SI = 2 * I
P = 128
NT = T // P
QB = 512
NB = T // QB
J = NH // NKV
HI = I // 2
CH = H // P
UNITS = NB * NKV
NFILL = 8
MROWS = 3
NBLK = 160
SLOTS = NBLK * P
STEP = 8
ROWS = T * K
RW = H + 1
EPS = 1e-5
TWO_ONES = float(np.array([0x3F803F80], np.uint32).view(np.float32)[0])
BIG = -1.0e30


def preln_attention_moe(nc, x, w_qkv, b_q, b_k, b_v, b_o, w_o, gate, w_sh1, w_sh2, w1, w2, trig, cst, out):
    f32, bf16, i32, u32 = mybir.dt.float32, mybir.dt.bfloat16, mybir.dt.int32, mybir.dt.uint32
    ALU, ACT, AX = mybir.AluOpType, mybir.ActivationFunctionType, mybir.AxisListType
    ds = bass.ds

    q_d = nc.dram_tensor("rotated_q", [NB, J, NKV, HD, QB], bf16).ap()
    k_d = nc.dram_tensor("rotated_k", [NB, NKV, HD, QB], bf16).ap()
    xs_d = nc.dram_tensor("slot_rows", [SLOTS, RW], f32).ap()
    y_d = nc.dram_tensor("expert_rows", [ROWS, H], f32).ap()

    ctx = ExitStack()
    with ctx:
        def sb(name, shape, dt=f32):
            return ctx.enter_context(nc.sbuf_tensor(name, shape, dt))

        def sem(name):
            return ctx.enter_context(nc.semaphore(name))

        x_sb = sb("x_sb", [P, NT * H])
        wqkv = sb("wqkv", [P, CH, 384])
        bq, bk = sb("bq", [P, 2]), sb("bk", [64, 1])
        bv, bo = sb("bv", [P, NKV * HD]), sb("bo", [P, H])
        wo = sb("wo", [P, NKV, H])
        gate_sb = sb("gate_sb", [P, CH, E])
        sh1 = sb("sh1", [P, CH, 2 * SI])
        sh2 = sb("sh2", [HI, 4, H])
        c_sb = sb("c_sb", [P, cst.shape[1]])
        ident = c_sb[:, 0:128]
        qmask = c_sb[:, 128:640]
        kmask = c_sb[:, 640:768]
        iota_e = c_sb[:, 768:832]
        tri_before = c_sb[0:E, 832:896]
        tri_upto = c_sb[0:E, 896:960]
        blk_start = c_sb[0:E, 960:960 + NBLK]
        ones_col = c_sb[0:E, 1120:1121]
        zero = sb("zero", [P, 1])
        ident16 = sb("ident16", [P, P], bf16)
        kmask16 = sb("kmask16", [P, P], bf16)
        stats = sb("stats", [P, NT, 6])
        mv = sb("mv", [P, NT * 2])
        rstd = sb("rstd", [P, NT])
        rs_tmp = sb("rs_tmp", [P, 2, NT])
        xn = sb("xn", [P, 4, H])
        xnT = sb("xnT", [P, CH, QB])
        q_aug = sb("q_aug", [P, UNITS, QB], bf16)
        k_pad = sb("k_pad", [P, J, NKV * T], bf16)
        v_all = sb("v_all", [P, NKV * NT * 32])
        v_cur = sb("v_cur", [P, NT, 32])
        p_ring = sb("p_ring", [P, 8, QB])
        o_nrm = sb("o_nrm", [P, UNITS * QB])
        cos, sin = o_nrm[:, 0:T], o_nrm[:, T:2 * T]
        rot = o_nrm[:, 2 * T:4 * T].bitcast(bf16).rearrange("p (a t) -> p a t", a=4)
        xn2T = sb("xn2T", [P, CH, T])
        m_part = sb("m_part", [P, 16, NB])
        m_row, m_neg, m_r1, m_r2 = sb("m_row", [P, 16]), sb("m_neg", [P, 16]), sb("m_r1", [P, 16]), sb("m_r2", [P, 16])
        m_stage = sb("m_stage", [P, 4, P], bf16)
        xn_flat = xn[:, :, :].rearrange("p n h -> p (n h)")
        scale, fill = xn_flat[:, 0:QB], xn_flat[:, QB:QB + RW]
        heads2 = xnT[:, :, :].rearrange("p c t -> p (c t)")
        scale_row = wqkv[:, :, :].rearrange("p c n -> p (c n)")[:, 0:QB]
        sums, inv_sums = sb("sums", [P, 16]), sb("inv_sums", [P, 16])
        places = {"k_pad": [k_pad[:, :, :].rearrange("p a b -> p (a b)").bitcast(f32), 0, J * NKV * T // 2],
                  "o_nrm": [o_nrm[:, :], 0, UNITS * QB],
                  "p_ring": [p_ring[:, :, :].rearrange("p a b -> p (a b)"), 0, 8 * QB],
                  "q_aug": [q_aug[:, :, :].rearrange("p a b -> p (a b)").bitcast(f32), 0, UNITS * QB // 2]}

        def lt(n, dt=f32, rows=P, where="k_pad"):
            ap, at, size = places[where]
            places[where][1] += n
            assert at + n <= size, where
            return ap[0:rows, at:at + n] if dt == f32 else ap[0:rows, at:at + n].bitcast(dt)

        hs = lt(4 * QB, rows=HI).rearrange("p (m t) -> p m t", m=4)
        hot = lt(NT * K * E // 2, bf16)
        hot_v = hot.rearrange("p (n k e) -> p n k e", n=NT, k=K)
        cum, spare, ones_row = lt(T, rows=E), lt(T), lt(T, rows=E)
        hotT = spare[0:E, :]
        stage = [lt(K * RW, where="o_nrm").rearrange("p (k w) -> p k w", k=K) for _ in range(2)]
        xn2_all = p_ring[:, :, :].rearrange("p a b -> p (a b)")
        lg = [xn_flat[:, h * 8 * E:(h + 1) * 8 * E] for h in range(2)]
        ex = [xnT[:, h, :] for h in range(2)]
        pr = lt(8 * E)
        row8, sum8, sum6 = [lt(8) for _ in range(2)], lt(8), lt(8)
        top8, idx8, idxf = lt(64), lt(64, u32), lt(64)
        wts = lt(NT * K)
        slot, slot_i = lt(NT * K), lt(NT * K, i32)
        row_i, row_f = lt(NT * K, i32), lt(NT * K)
        cnt = lt(8, rows=E)
        past_end = lt(NBLK, rows=E)
        eob = lt(NBLK, i32, rows=1)
        sg = lt(2 * QB, rows=HI).rearrange("p (a t) -> p a t", a=2)
        w1s = [lt(CH * I, where="q_aug").rearrange("p (c i) -> p c i", c=CH) for _ in range(4)]
        w2s = [lt(2 * H, rows=HI, where="q_aug").rearrange("p (c n) -> p c n", c=2) for _ in range(4)]
        ids_y = [lt(1, i32) for _ in range(STEP)]
        xg, ys = [lt(RW, where="o_nrm") for _ in range(STEP)], [spare[:, n * H:(n + 1) * H] for n in range(STEP)]
        xgT = [lt(H, where="o_nrm") for _ in range(2)]
        hT = [lt(2 * P, rows=HI, where="o_nrm") for _ in range(2)]
        prod = o_nrm[:, UNITS * QB - NT * K * E // 2:]
        yk = [o_nrm[:, n * K * H:(n + 1) * K * H] for n in range(4)]
        acc = [o_nrm[:, 4 * K * H + n * H:4 * K * H + (n + 1) * H] for n in range(4)]

        bank = [ctx.enter_context(nc.psum_tensor(f"bank{n}", [P, 512], f32)) for n in range(8)]
        bank16 = [b[:, :].bitcast(bf16) for b in bank]
        S_Q = bank[0:4]
        S_K = bank[4:6]
        C_BANKS = [bank[n] for n in (0, 1, 6, 7)]
        PV = bank[6]

        passed = sem("passed")
        ld_x = [sem(f"ld_x{n}") for n in range(4)]
        (ld_w, ld_qkv, k_ones, rot_stored, zero_set, ld_c, ld_late, consts16, q_zeroed, k_zeroed,
         v_ones, dve, pool) = map(sem, (
            "ld_w", "ld_qkv", "k_ones", "rot_stored", "zero_set", "ld_c", "ld_late", "consts16", "q_zeroed", "k_zeroed",
            "v_ones", "dve_chain", "pool_chain"))
        (xn_ready, xn_used, xnT_ready, q_mm, k_mm, v_mm, rot_terms, rot_done, qk_placed, v_done) = map(sem, (
            "xn_ready", "xn_used", "xnT_ready", "q_mm", "k_mm", "v_mm", "rot_terms", "rot_done",
            "qk_placed", "v_done"))
        (sq_ready, sq_used, sk_ready, p_ready, pv_done, v_staged, max_ready, split_done, mT_ready,
         mrow_placed, o_done, pv_copied, sums_moved, inverted, inv_moved, scale_ready,
         scale_row_set, xb_done) = map(sem, (
            "sq_ready", "sq_used", "sk_ready", "p_ready", "pv_done", "v_staged", "max_ready", "split_done",
            "mT_ready", "mrow_placed", "o_done", "pv_copied", "sums_moved", "inverted",
            "inv_moved", "scale_ready", "scale_row_set", "xb_done"))
        (wo_mm, x1_done, xn2_ready, xn2_used, xn2T_ready, logit_mm, logit_sub,
         exp_done, hot_ready) = map(sem, (
            "wo_mm", "x1_done", "xn2_ready", "xn2_used", "xn2T_ready",
            "logit_mm", "logit_sub", "exp_done", "hot_ready"))
        (hot_mm, hotT_done, late_consts, padded, base_mm, slotT_ready, slotT_mm, past_ready, eob_mm,
         eob_ready, slot_ready, filled, fill_set, staged) = map(sem, (
            "hot_mm", "hotT_done", "late_consts", "padded", "base_mm", "slotT_ready", "slotT_mm",
            "past_ready", "eob_mm", "eob_ready", "slot_ready", "filled", "fill_set", "staged"))
        scattered = [sem(f"scattered{n}") for n in range(2)]
        (sh_mm, sg_ready, hs_ready, shd_mm, sh_added) = map(sem, (
            "sh_mm", "sg_ready", "hs_ready", "shd_mm", "sh_added"))
        w_loaded = [sem(f"w_loaded{n}") for n in range(4)]
        xg_loaded = [sem(f"xg_loaded{n}") for n in range(STEP)]
        y_stored = [sem(f"y_stored{n}") for n in range(STEP)]
        (idy_ready, xg_T, xgT_ready, up_mm, h_ready, down_mm, y_ready, summed) = map(sem, (
            "idy_ready", "xg_T", "xgT_ready", "up_mm", "h_ready", "down_mm", "y_ready", "summed"))
        yk_loaded = [sem(f"yk_loaded{n}") for n in range(4)]
        out_stored = [sem(f"out_stored{n}") for n in range(4)]

        def wait(eng, s, value):
            if not isinstance(value, int) or value > 0:
                eng.wait_ge(s, value)

        def wait_apart(eng, s, value):
            wait(eng, s, value)
            if not isinstance(value, int):
                eng.sem_inc(passed, 1)

        class Chain:

            def __init__(self, eng, s):
                self.eng, self.s, self.base, self.n = eng, s, 0, 0

            def link(self, ins):
                self.n += 1
                ins.then_inc(self.s, 1)
                wait_apart(self.eng, self.s, self.base + self.n)

            def enter(self, step, per):
                self.start, self.per = self.base + self.n, per
                self.base, self.n = step * per + self.start, 0

            def leave(self, steps):
                assert self.n == self.per
                self.base, self.n = self.start + steps * self.per, 0

        def key_tiles(b):
            return 4 * (b + 1)

        def tiles_before(b, g):
            return g * key_tiles(b) + 8 * b * (b + 1)

        def maxes_before(b, g):
            return g * (16 * (b + 1)) + 32 * b * (b + 1)

        def max_chunks(b):
            return [(tt, c, j) for tt in range(4) for c in range(b + 1) for j in range(J)]

        def chunks_beside(b, mb):
            widths = [QB + 256 - P * max(0, st - 4 * b) for st in range(key_tiles(b))]
            costs = [QB + 64 if c < mb else P * (tt + 1) + 64 for tt, c, _ in max_chunks(mb)]
            beside, n, done = [], 0, 0
            for st in range(len(widths)):
                start = n
                while n < len(costs) and (done + costs[n]) * sum(widths) <= sum(widths[:st + 1]) * sum(costs):
                    done += costs[n]
                    n += 1
                beside.append(range(start, n))
            return beside

        def sk_bank(mb, n):
            return S_K[n % 2] if mb is not None else (S_K + S_Q)[n % 4]

        def bodies(eng, body):
            for g in range(2):
                body(0, g, 0, g + 2, g)
            for b in range(NB):
                if b:
                    with eng.Fori(0, 2) as g:
                        body(b, g, b, g + 2, g)
                if b == 0:
                    for g in range(2):
                        body(b, g + 2, b + 1, g, g)
                elif b + 1 < NB:
                    with eng.Fori(0, 2) as g:
                        body(b, g + 2, b + 1, g, g)
            for g in range(2):
                body(NB - 1, g + 2, None, g, g)

        def heads_of(odd):
            return heads2[:, ds(odd * QB, QB)]

        def has_next(mb, mg):
            return mb is not None or mg == 0

        block = ctx.enter_context(nc.Block())

        @block.sync
        def _(sp):
            xt = x.rearrange("o (n p) h -> p (o n) h", p=P)
            xv = x_sb[:, :].rearrange("p (n h) -> p n h", h=H)
            sp.dma_start(xv[:, 0:4, :], xt[:, 0:4, :]).then_inc(ld_x[0], 16)
            sp.dma_start(c_sb[:, :], cst).then_inc(ld_c, 16)
            sp.dma_start(wqkv[:, :, :], w_qkv).then_inc(ld_qkv, 16)
            for n in range(1, 4):
                sp.dma_start(xv[:, 4 * n:4 * n + 4, :], xt[:, 4 * n:4 * n + 4, :]).then_inc(ld_x[n], 16)
            sp.dma_start(bq[:, :], b_q).then_inc(ld_w, 16)
            sp.dma_start(bk[:, :], b_k).then_inc(ld_w, 16)
            sp.dma_start(bv[:, :], b_v).then_inc(ld_w, 16)
            sp.dma_start(bo[:, :], b_o).then_inc(ld_w, 16)
            sp.dma_start(o_nrm[:, 0:2 * T], trig).then_inc(ld_w, 16)
            sp.dma_start(wo[:, :, :], w_o).then_inc(ld_late, 16)
            sp.dma_start(gate_sb[:, :, :], gate).then_inc(ld_late, 16)
            sp.dma_start(sh1[:, :, :], w_sh1).then_inc(ld_late, 16)
            sp.dma_start(sh2[:, :, :], w_sh2).then_inc(ld_late, 16)
            sp.wait_ge(q_zeroed, 1)
            sp.wait_ge(k_ones, 1)
            sp.sem_inc(qk_placed, 32 * J)
            with sp.Fori(0, NB) as b:
                sp.wait_ge(rot_done, b * 4 + 8)
                sp.dma_start(q_d[ds(b, 1)].rearrange("b j g (i a) t -> (b j g i) a t", a=2),
                             rot[:, 0:2, ds(b * QB, QB)]).then_inc(rot_stored, 16)
                sp.dma_start(k_d[ds(b, 1)].rearrange("b g (i a) t -> (b g i) a t", a=2),
                             rot[0:32, 2:4, ds(b * QB, QB)]).then_inc(rot_stored, 16)
                sp.wait_ge(rot_stored, b * 32 + 32)
                sp.wait_ge(qk_placed, b * (32 * J) + 32 * J)
                for j in range(J):
                    rows = slice(32 * j + MROWS, 32 * j + MROWS + HD)
                    sp.dma_start(q_aug[rows, ds(b * NKV, NKV), :],
                                 q_d[ds(b, 1), j].rearrange("b g r t -> (b r) g t")).then_inc(qk_placed, 16)
                    sp.dma_start(k_pad[rows, j, :].rearrange("p (g t) -> p g t", g=NKV)[:, :, ds(b * QB, QB)],
                                 k_d[ds(b, 1)].rearrange("b g r t -> (b r) g t")).then_inc(qk_placed, 16)

            def sums_out(u, odd):
                wait_apart(sp, pv_copied, u + 1)
                wait(sp, inverted, u)
                for j in range(J):
                    sp.dma_start(sums[32 * j:32 * j + 32, :],
                                 heads2[32 * j + HD:32 * j + HD + 1, ds(odd * QB, QB)].rearrange("p (r c) -> p r c", c=16)).then_inc(sums_moved, 16)

            def inverses_back(u):
                wait_apart(sp, inverted, u + 1)
                wait(sp, scale_ready, u)
                for j in range(J):
                    sp.dma_start(scale_row[32 * j:32 * j + 1, :].rearrange("p (r c) -> p r c", c=16),
                                 inv_sums[32 * j:32 * j + 32, :]).then_inc(inv_moved, 16)

            def body(b, g, mb, mg, odd):
                if not (isinstance(g, int) and b + g == 0):
                    sums_out(g + (4 * b - 1), odd * -1 + 1)
                    inverses_back(g + (4 * b - 1))

            sp.wait_ge(scale_row_set, 1)
            bodies(sp, body)
            sums_out(UNITS - 1, 1)
            inverses_back(UNITS - 1)

            sp.wait_ge(eob_ready, 1)

            def load_weights(it, s):
                expert = sp.value_load(eob[0:1, ds(it * STEP + s, 1)], min_val=0, max_val=E - 1)
                sp.wait_ge(down_mm, it * STEP + (s + 1))
                sp.dma_start(w1s[s % 4].unsqueeze(1), w1[:, ds(expert, 1), :, :]).then_inc(w_loaded[s % 4], 16)
                sp.dma_start(w2s[s % 4].unsqueeze(1), w2[:, ds(expert, 1), :, :]).then_inc(w_loaded[s % 4], 16)

            with sp.Fori(0, NBLK // STEP) as it:
                for s in range(STEP):
                    load_weights(it, s)
            for s in range(STEP):
                sp.wait_ge(y_stored[s], 16 * (NBLK // STEP))
            y_t = y_d.rearrange("(n p k) h -> p n (k h)", p=P, k=K)
            with sp.Fori(0, NT // 4) as it:
                for h in range(4):
                    sp.wait_ge(summed, it * 4 + (h + 1))
                    sp.dma_start(yk[h].unsqueeze(1), y_t[:, ds(it * 4 + h, 1), :]).then_inc(yk_loaded[h], 16)

        @block.gpsimd
        def _(gp):
            chain = Chain(gp, pool)
            gp.sem_inc(rot_done, 4)
            nc.gpsimd.memset(v_all[:, :], 16.0).then_inc(v_ones, 1)
            chain.link(nc.gpsimd.memset(m_stage[:, :, :], 0.0))
            for j in range(J):
                gp.wait_ge(k_zeroed, j + 1)
                chain.link(nc.gpsimd.memset(k_pad[32 * j:32 * j + MROWS, j, :].bitcast(f32), TWO_ONES))
            gp.sem_inc(k_ones, 1)

            with gp.Fori(0, NB) as b:
                for n, op in enumerate((ALU.subtract, ALU.add, ALU.subtract, ALU.add)):
                    rows = P if n < 2 else 32
                    gp.wait_ge(rot_terms, b * 8 + (2 * n + 2))
                    nc.gpsimd.tensor_tensor(rot[0:rows, n, ds(b * QB, QB)], p_ring[0:rows, 2 * n, :],
                                            p_ring[0:rows, 2 * n + 1, :], op).then_inc(rot_done, 1)

            def stage_v(b, g):
                nst, before = key_tiles(b), tiles_before(b, g)
                for st in range(nst):
                    wait_apart(gp, pv_done, before + (st + 1 - nst))
                    nc.gpsimd.tensor_copy(v_cur[:, nst - 1 - st, :], v_all[:, ds(g * (NT * 32) + st * 32, 32)]).then_inc(v_staged, 1)

            def split(u):
                part = [m_stage[:, :, :].rearrange("p t (j r) -> p t j r", j=J)[:, :, :, r] for r in range(MROWS)]
                neg, r1, r2 = (t[:, :].rearrange("p (t j) -> p t j", t=4) for t in (m_neg, m_r1, m_r2))
                gp.wait_ge(max_ready, u + 1)
                wait_apart(gp, mT_ready, u)
                chain.link(nc.gpsimd.tensor_scalar(m_neg[:, :], m_row[:, :], -1.0, None, ALU.mult))
                chain.link(nc.gpsimd.tensor_copy(part[0], neg))
                chain.link(nc.gpsimd.tensor_tensor(r1, neg, part[0], ALU.subtract))
                chain.link(nc.gpsimd.tensor_copy(part[1], r1))
                chain.link(nc.gpsimd.tensor_tensor(r2, r1, part[1], ALU.subtract))
                nc.gpsimd.tensor_copy(part[2], r2).then_inc(split_done, 1)

            def normalise(u, odd):
                gp.wait_ge(scale_ready, u + 1)
                nc.gpsimd.tensor_tensor(o_nrm[:, ds(u * QB, QB)], heads_of(odd), scale, ALU.mult).then_inc(o_done, 1)

            def body(b, g, mb, mg, odd):
                if has_next(mb, mg):
                    chain.base, chain.n = g * 5 + (split_links + 5 * (4 * b + 1)), 0
                    split(g + (4 * b + 1))
                stage_v(b, g)
                if not (isinstance(g, int) and 4 * b + g < 2) and (mb is not None or mg == 0):
                    normalise(g + (4 * b - 2), odd)
                if mb is None:
                    normalise(g + (4 * b - 1), 1 - odd)

            gp.wait_ge(v_done, NB + 1)
            gp.wait_ge(xn_ready, NT)
            gp.wait_ge(ld_w, 16 * 5)
            for n in range(NT):
                nc.gpsimd.tensor_tensor(x_sb[:, n * H:(n + 1) * H], x_sb[:, n * H:(n + 1) * H], bo[:, :], ALU.add
                                        ).then_inc(xb_done, 1)
            split_links = chain.n
            split(0)
            bodies(gp, body)
            normalise(UNITS - 1, 1)
            chain.base, chain.n = split_links + 5 * UNITS, 0

            gp.wait_ge(pv_done, tiles_before(NB - 1, NKV))
            nc.gpsimd.memset(ones_row, 1.0)
            nc.gpsimd.iota(row_i.rearrange("p (n k) -> p n k", k=K), [[P * K, NT], [1, K]], base=0, channel_multiplier=K
                           ).then_inc(late_consts, 1)
            gp.wait_ge(late_consts, 1)
            nc.gpsimd.tensor_copy(row_f, row_i).then_inc(late_consts, 1)
            gp.wait_ge(filled, 16 * NFILL)
            gp.wait_ge(slot_ready, 1)
            for n in range(NT):
                gp.wait_ge(staged, n + 1)
                for k in range(K):
                    at = n * K + k
                    gp.indirect_dma_start(
                        out=xs_d[:, :], out_offset=bass.IndirectOffsetOnAxis(ap=slot_i.bitcast(u32)[:, at:at + 1], axis=0),
                        in_=stage[n % 2][:, k, :], in_offset=None).then_inc(scattered[n % 2], 16)

            def scatter(it, s):
                gp.wait_ge(idy_ready, it * STEP + (s + 1 + STEP))
                wait_apart(gp, y_ready, it * STEP + (s + 3))
                gp.indirect_dma_start(
                    out=y_d[:, :], out_offset=bass.IndirectOffsetOnAxis(ap=ids_y[s].bitcast(u32), axis=0),
                    in_=ys[s], in_offset=None, bounds_check=ROWS - 1, oob_is_err=False).then_inc(y_stored[s], 16)

            with gp.Fori(0, NBLK // STEP) as it:
                for s in range(STEP):
                    scatter(it, s)

        @block.scalar
        def _(act):
            act.wait_ge(zero_set, 1)
            for j in range(J):
                nc.scalar.copy(k_pad[:, j, :].bitcast(f32), zero[:, :].to_broadcast([P, NKV * T // 2])).then_inc(k_zeroed, 1)
            act.sem_inc(xnT_ready, 2)
            with act.Fori(0, NB) as b:
                act.wait_ge(xn_used, b * 4 + 8)
                act.wait_ge(v_mm, b + 1)
                for c in range(CH):
                    nc.scalar.copy(xnT[:, c, :], bank[c][:, :]).then_inc(xnT_ready, 1)

            def place_max_rows(u, j):
                act.wait_ge(mT_ready, u + 1)
                rows = slice(32 * j, 32 * j + MROWS)
                nc.scalar.copy(q_aug[rows, ds(u, 1), :].rearrange("p u t -> p (u t)"), bank16[7][rows, 0:QB]
                               ).then_inc(mrow_placed, 1)

            xs_fill = xs_d.rearrange("(b p) w -> p b w", p=P)
            act.wait_ge(fill_set, 1)
            act.wait_ge(rot_done, NB * 4 + 4)

            def body(b, g, mb, mg, odd):
                before = tiles_before(b, g)
                for st in range(key_tiles(b)):
                    if st == key_tiles(b) // 2:
                        if b >= NB - NFILL // NKV:
                            n = NBLK // NFILL
                            act.dma_start(xs_fill[:, ds(g * n + (b - NB + NFILL // NKV) * (NKV * n), n), :],
                                          fill.unsqueeze(1).to_broadcast([P, n, RW])).then_inc(filled, 16)
                    at = 128 * max(0, st - 4 * b)
                    for j in range(J):
                        chunk = 4 * st + j
                        act.wait_ge(sk_ready, before * 4 + (chunk + 1))
                        if j == 0:
                            wait(act, pv_done, before + (st - 1))
                        nc.scalar.activation(p_ring[:, chunk % 8, at:QB], sk_bank(mb, chunk)[:, at:QB], ACT.Exp).then_inc(p_ready, 1)
                        if st == key_tiles(b) // 2 and has_next(mb, mg):
                            place_max_rows(g + (4 * b + 1), j)
                    if st == 0:
                        copy_heads(before, g + (4 * b - 1), odd * -1 + 1)

            def copy_heads(tiles, u, odd):
                wait(act, pv_done, tiles)
                wait(act, o_done, u - 1)
                if not isinstance(u, int) or u >= 0:
                    nc.scalar.copy(heads_of(odd), PV[:, :]).then_inc(pv_copied, 1)

            for j in range(J):
                place_max_rows(0, j)
            bodies(act, body)
            copy_heads(tiles_before(NB - 1, NKV), UNITS - 1, 1)

            for b in range(NB):
                act.wait_ge(xn2_used, b + 1)
                for c in range(CH):
                    nc.scalar.copy(xn2T[:, c, b * QB:(b + 1) * QB], bank[2 + 2 * (b % 2) + c][:, :]).then_inc(xn2T_ready, 1)
            for h in range(2):
                act.wait_ge(logit_sub, h + 1)
                nc.scalar.activation(ex[h], lg[h], ACT.Exp).then_inc(exp_done, 1)
            for n in range(4):
                act.wait_ge(hot_mm, n + 1)
                nc.scalar.copy(hotT[:, n * QB:(n + 1) * QB], bank[n][0:E, :]).then_inc(hotT_done, 1)

            def stage_tile(b, m):
                if not isinstance(b, int) or 4 * b + m >= 2:
                    act.wait_ge(scattered[m % 2], b * (32 * K) + m // 2 * (16 * K))
                nc.scalar.copy(stage[m % 2][:, :, 0:H], xn2_all[:, ds(b * (4 * H) + m * H, H)].unsqueeze(1).to_broadcast([P, K, H]))
                nc.scalar.copy(stage[m % 2][:, :, H], row_f[:, ds(b * (4 * K) + m * K, K)]).then_inc(staged, 1)

            def gates_and_tiles(b, more):
                for m in range(4):
                    act.wait_ge(sh_mm, b * 4 + (m + 1))
                    act.wait_ge(hs_ready, b * 4 + (m + 1))
                    nc.scalar.activation(sg[:, m % 2, :], bank[m % 2][0:HI, :], ACT.Silu).then_inc(sg_ready, 1)
                    if m == 0:
                        stage_tile(b, 2)
                    if m == 2:
                        stage_tile(b, 3)
                if more:
                    stage_tile(b + 1, 0)
                    stage_tile(b + 1, 1)

            act.wait_ge(late_consts, 2)
            act.wait_ge(xn2_ready, NT)
            stage_tile(0, 0)
            stage_tile(0, 1)
            gates_and_tiles(0, True)
            with act.Fori(1, NB - 1) as b:
                gates_and_tiles(b, True)
            gates_and_tiles(NB - 1, False)

            xs_v = xs_d.rearrange("(b p) w -> p b w", p=P)
            for h in range(2):
                act.wait_ge(scattered[h], 16 * NT * K // 2)

            def load_rows(it, s):
                act.wait_ge(idy_ready, it * STEP + (s + 1))
                act.dma_start(xg[s].unsqueeze(1), xs_v[:, ds(it * STEP + s, 1), :]).then_inc(xg_loaded[s], 16)

            def silu(it, s):
                act.wait_ge(up_mm, it * STEP + (s + 3))
                act.wait_ge(down_mm, it * STEP + (s + 3))
                nc.scalar.activation(hT[s % 2], bank[2 + s % 2][0:HI, 0:2 * P], ACT.Silu).then_inc(h_ready, 1)

            def copy_y(it, s):
                act.wait_ge(down_mm, it * STEP + (s + 5))
                wait(act, y_stored[s], it * 16)
                nc.scalar.copy(ys[s], bank[4 + s % 2][:, 0:H]).then_inc(y_ready, 1)

            act.sem_inc(h_ready, 2)
            act.sem_inc(y_ready, 2)
            for s in range(6):
                load_rows(0, s)
            silu(0, 0)

            def silu_and_copy(it):
                for s in range(STEP):
                    silu(it + (s + 1) // STEP, (s + 1) % STEP)
                    load_rows(it + (s + 6) // STEP, (s + 6) % STEP)
                    copy_y(it, s)

            silu_and_copy(0)
            with act.Fori(1, NBLK // STEP - 1) as it:
                silu_and_copy(it)
            for s in range(STEP):
                if s < STEP - 1:
                    silu(NBLK // STEP - 1, s + 1)
                if s < STEP - 6:
                    load_rows(NBLK // STEP - 1, s + 6)
                copy_y(NBLK // STEP - 1, s)
            for h in range(4):
                act.sem_inc(out_stored[h], 16)
            out_t = out.rearrange("o (n p) h -> p (o n) h", p=P)
            with act.Fori(0, NT // 4) as it:
                for h in range(4):
                    act.wait_ge(summed, it * 4 + (h + 5))
                    act.dma_start(out_t[:, ds(it * 4 + h, 1), :], acc[h].unsqueeze(1)).then_inc(out_stored[h], 16)
            for h in range(4):
                act.wait_ge(out_stored[h], 16 * (NT // 4) + 16)

        @block.vector
        def _(v):
            chain = Chain(v, dve)
            link = chain.link
            nc.vector.memset(zero[:, :], 0.0).then_inc(zero_set, 1)
            nc.vector.memset(q_aug[:, :, :].rearrange("p a b -> p (a b)").bitcast(f32), 0.0).then_inc(q_zeroed, 1)
            v.wait_ge(ld_c, 16)
            nc.vector.tensor_copy(ident16[:, :], ident)
            nc.vector.tensor_copy(kmask16[:, :], kmask).then_inc(consts16, 1)

            def inv_sqrt(n, at=0):
                var, y, y2, half = mv_all[:, at:at + n, 1], rstd[:, at:at + n], rs_tmp[:, 0, 0:n], rs_tmp[:, 1, 0:n]
                link(nc.vector.tensor_scalar(half, var, EPS, None, ALU.add))
                link(nc.vector.tensor_scalar(y2.bitcast(i32), half.bitcast(i32), 1, None, ALU.logical_shift_right))
                nc.vector.tensor_scalar(half, half, 0.5, None, ALU.mult)
                link(nc.vector.tensor_scalar(y.bitcast(i32), y2.bitcast(i32), -1.0, float(0x5F3759DF), ALU.mult, ALU.add))
                for _ in range(3):
                    link(nc.vector.scalar_tensor_tensor(y2, y, -1.0, y, ALU.mult, ALU.mult))
                    link(nc.vector.tensor_tensor(y2, y2, half, ALU.mult))
                    link(nc.vector.scalar_tensor_tensor(y, y2, 1.5, y, ALU.add, ALU.mult))

            mv_all = mv[:, :].rearrange("p (n w) -> p n w", w=2)

            def statistics(tiles):
                for n in tiles:
                    if n % 4 == 0:
                        v.wait_ge(ld_x[n // 4], 16)
                    last = nc.vector.bn_stats(stats[:, n, :], x_sb[:, n * H:(n + 1) * H])
                link(last)
                for n in tiles:
                    last = nc.vector.bn_aggr(mv[:, 2 * n:2 * n + 2], stats[:, n, :])
                link(last)
                inv_sqrt(len(tiles), tiles[0])

            def normalise_rows(b, used):
                wait(v, xn_used, used)
                for tt in range(4):
                    nc.vector.tensor_scalar(xn[:, tt, :], x_sb[:, ds(b * (4 * H) + tt * H, H)], mv[:, ds(b * 8 + 2 * tt, 1)],
                                            rstd[:, ds(b * 4 + tt, 1)], ALU.subtract, ALU.mult).then_inc(xn_ready, 1)

            v_rows = v_all[:, :].rearrange("p (g m) -> p g m", g=NKV)

            def biases_and_rotation(b):
                for part, (mm, rows, even, odd) in enumerate((
                        (q_mm, P, (bank[2], slice(0, P), bq[:, 0:1]), (bank[3], slice(0, P), bq[:, 1:2])),
                        (k_mm, 32, (bank[4], slice(0, 32), bk[0:32, :]), (bank[4], slice(32, 64), bk[32:64, :])))):
                    v.wait_ge(rot_done, b * 4 + (2 * part + 2))
                    v.wait_ge(mm, b + 1)
                    for n, ((src, at, bias), tabl) in enumerate(((even, cos), (odd, sin), (even, sin), (odd, cos))):
                        nc.vector.scalar_tensor_tensor(p_ring[0:rows, 4 * part + n, :], src[at, :], bias,
                                                       tabl[at, ds(b * QB, QB)], ALU.add, ALU.mult).then_inc(rot_terms, 1)
                v.wait_ge(v_mm, b + 2)
                v_ps = bank[6][:, 0:4 * NKV * HD].rearrange("p (n g d) -> p n g d", n=4, g=NKV)
                bv_g = bv[:, :].rearrange("p (g d) -> p g d", g=NKV)
                for tt in range(4):
                    last = nc.vector.tensor_tensor(v_rows[:, :, ds(b * 128 + tt * 32, HD)], v_ps[:, tt, :, :], bv_g, ALU.add)
                last.then_inc(v_done, 1)

            statistics(range(4))
            normalise_rows(0, 0)
            statistics(range(4, NT))
            v.wait_ge(ld_w, 16 * 5)
            v.wait_ge(v_ones, 1)
            v.sem_inc(v_done, 1)
            with v.Fori(0, NB - 1) as b:
                normalise_rows(b + 1, b * 4 + 8)
                biases_and_rotation(b)
            biases_and_rotation(NB - 1)

            nc.vector.memset(scale_row, 1.0).then_inc(scale_row_set, 1)
            v.wait_ge(xn_used, NT + 4)
            nc.vector.memset(fill, float(ROWS)).then_inc(fill_set, 1)

            def row_max(b, g, n):
                tt, c, j = max_chunks(b)[n]
                src = S_Q[n % 4]
                at = m_part[:, tt * J + j, c:c + 1]
                if c < b:
                    v.wait_ge(sq_ready, maxes_before(b, g) + (n + 1))
                    nc.vector.reduce_max(at, src[:, :], AX.X).then_inc(sq_used, 1)
                else:
                    w = 128 * (tt + 1)
                    wait_apart(v, sq_ready, maxes_before(b, g) + (n + 1))
                    nc.vector.tensor_tensor_reduce(out=src[:, 0:w], in0=src[:, 0:w], in1=qmask[:, 512 - w:512], scale=1.0,
                                                   scalar=-3.0e38, op0=ALU.add, op1=ALU.max, accum_out=at).then_inc(sq_used, 1)

            def row_max_all(b, g, u, between=None):
                wait_apart(v, max_ready, u)
                for n in range(16 * (b + 1)):
                    row_max(b, g, n)
                    if between:
                        between(n + 1)
                v.wait_ge(sq_used, maxes_before(b, g) + 16 * (b + 1))
                wait(v, split_done, u)
                nc.vector.reduce_max(m_row[:, :], m_part[:, :, 0:b + 1], AX.X).then_inc(max_ready, 1)

            def invert_sums(u):
                v.wait_ge(sums_moved, (u + 1) * (16 * J))
                nc.vector.reciprocal(inv_sums[:, :], sums[:, :]).then_inc(inverted, 1)

            def spread_scale(u):
                v.wait_ge(inv_moved, (u + 1) * (16 * J))
                wait_apart(v, o_done, u)
                nc.vector.stream_shuffle(scale, scale_row, [0] * 32).then_inc(scale_ready, 1)

            def body(b, g, mb, mg, odd):
                first, u = isinstance(g, int) and b == 0, g + 4 * b
                if mb is None:
                    if mg == 0:
                        spread_scale(u - 2)
                    invert_sums(u - 1)
                    spread_scale(u - 1)
                    return

                def between(n):
                    if n == 6 * (mb + 1) and not (first and g < 2):
                        spread_scale(u - 2)

                row_max_all(mb, mg, u + 2, between)
                if not (first and g < 1):
                    invert_sums(u - 1)

            row_max_all(0, 0, 0)
            row_max_all(0, 1, 1)
            bodies(v, body)

            def residual(n):
                xs = x_sb[:, n * H:(n + 1) * H]
                v.wait_ge(wo_mm, n + 1)
                nc.vector.tensor_tensor(xs, C_BANKS[n % 4][:, 0:H], xs, ALU.add).then_inc(x1_done, 1)
                if n % 8:
                    statistics2(n - 1)

            def statistics2(n):
                v.wait_ge(x1_done, n + 1)
                return nc.vector.bn_stats(stats[:, n, :], x_sb[:, n * H:(n + 1) * H])

            invert_sums(UNITS - 1)
            v.wait_ge(xb_done, NT)
            for n in range(4):
                residual(n)
            spread_scale(UNITS - 1)
            for h in range(2):
                tiles = range(8 * h, 8 * h + 8)
                for n in tiles:
                    if n >= 4:
                        residual(n)
                link(statistics2(8 * h + 7))
                for n in tiles:
                    last = nc.vector.bn_aggr(mv[:, 2 * n:2 * n + 2], stats[:, n, :])
                link(last)
                inv_sqrt(8, 8 * h)
                for n in tiles:
                    nc.vector.tensor_scalar(xn2_all[:, n * H:(n + 1) * H], x_sb[:, n * H:(n + 1) * H], mv[:, 2 * n:2 * n + 1],
                                            rstd[:, n:n + 1], ALU.subtract, ALU.mult).then_inc(xn2_ready, 1)
            def each(t):
                return t.rearrange("p (n e) -> p n e", n=8)

            v.wait_ge(filled, 16 * NFILL)
            for h in range(2):
                v.wait_ge(logit_mm, h + 1)
                logits = each(bank[6 + h][:, :])
                link(nc.vector.reduce_max(row8[h], logits, AX.X))
                nc.vector.tensor_tensor(each(lg[h]), logits, row8[h].unsqueeze(2).to_broadcast([P, 8, E]), ALU.subtract
                                        ).then_inc(logit_sub, 1)
            for h in range(2):
                v.wait_ge(exp_done, h + 1)
                link(nc.vector.reduce_sum(sum8, each(ex[h]), AX.X))
                link(nc.vector.reciprocal(sum8, sum8))
                link(nc.vector.tensor_tensor(each(pr), each(ex[h]), sum8.unsqueeze(2).to_broadcast([P, 8, E]), ALU.mult))
                for t in range(8):
                    last = nc.vector.max(top8[:, 8 * t:8 * t + 8], pr[:, E * t:E * t + E])
                link(last)
                for t in range(8):
                    last = nc.vector.max_index(idx8[:, 8 * t:8 * t + 8], top8[:, 8 * t:8 * t + 8], pr[:, E * t:E * t + E])
                link(last)
                link(nc.vector.reduce_sum(sum6, each(top8)[:, :, 0:K], AX.X))
                link(nc.vector.reciprocal(sum6, sum6))
                link(nc.vector.tensor_tensor(each(wts[:, h * 8 * K:(h + 1) * 8 * K]), each(top8)[:, :, 0:K],
                                             sum6.unsqueeze(2).to_broadcast([P, 8, K]), ALU.mult))
                link(nc.vector.tensor_copy(idxf, idx8))
                nc.vector.tensor_tensor(hot_v[:, 8 * h:8 * h + 8], iota_e.unsqueeze(1).unsqueeze(1).to_broadcast([P, 8, K, E]),
                                        each(idxf)[:, :, 0:K].unsqueeze(3).to_broadcast([P, 8, K, E]), ALU.is_equal
                                        ).then_inc(hot_ready, 1)

            v.wait_ge(hotT_done, 4)
            v.wait_ge(late_consts, 2)
            link(nc.vector.tensor_tensor_scan(cum, ones_row, hotT, 0.0, ALU.mult, ALU.add))
            c_int = cnt.bitcast(i32)
            link(nc.vector.tensor_scalar(c_int[:, 0:1], cum[:, T - 1:T], float(P - 1), None, ALU.add))
            link(nc.vector.tensor_scalar(c_int[:, 1:2], c_int[:, 0:1], -P, None, ALU.bitwise_and))
            nc.vector.tensor_copy(cnt[:, 2:3], c_int[:, 1:2]).then_inc(padded, 1)
            v.wait_ge(base_mm, 1)
            nc.vector.tensor_copy(cnt[:, 4:5], bank[5][0:E, 1:2])
            link(nc.vector.tensor_scalar(cnt[:, 3:4], bank[5][0:E, 0:1], -1.0, None, ALU.add))
            nc.vector.tensor_scalar(past_end, blk_start, cnt[:, 4:5], None, ALU.is_ge).then_inc(past_ready, 1)
            nc.vector.tensor_scalar(cum, cum, cnt[:, 3:4], None, ALU.add).then_inc(slotT_ready, 1)
            prod_v = prod.rearrange("p (n k e) -> p n k e", n=8, k=K)
            for h in range(2):
                v.wait_ge(slotT_mm, h + 1)
                slots = bank[6 + h][:, :].rearrange("p (n e) -> p n e", n=8).unsqueeze(2).to_broadcast([P, 8, K, E])
                link(nc.vector.tensor_tensor(prod_v, hot_v[:, 8 * h:8 * h + 8], slots, ALU.mult))
                link(nc.vector.reduce_sum(slot[:, h * 8 * K:(h + 1) * 8 * K].rearrange("p (n k) -> p n k", k=K), prod_v, AX.X))
            nc.vector.tensor_copy(slot_i, slot).then_inc(slot_ready, 1)
            v.wait_ge(eob_mm, 1)
            link(nc.vector.tensor_scalar(past_end[0:1, :], bank[5][0:1, 2:2 + NBLK], float(E - 1), None, ALU.min))
            nc.vector.tensor_copy(eob, past_end[0:1, :]).then_inc(eob_ready, 1)

            v.sem_inc(hs_ready, 2)
            v.sem_inc(sh_added, 2)
            with v.Fori(0, NB) as b:
                v.wait_ge(shd_mm, b * 4 + 4)
                for m in range(4):
                    v.wait_ge(sg_ready, b * 4 + (m + 1))
                    nc.vector.tensor_tensor(hs[:, m, :], bank[2 + m % 2][0:HI, :], sg[:, m % 2, :], ALU.mult).then_inc(hs_ready, 1)
                for tt in range(4):
                    xs = x_sb[:, ds(b * (4 * H) + tt * H, H)]
                    v.wait_ge(shd_mm, b * 4 + (tt + 5))
                    nc.vector.tensor_tensor(xs, bank[4 + tt % 2][:, 0:H], xs, ALU.add).then_inc(sh_added, 1)

            def rows_T(it, s):
                v.wait_ge(xg_T, it * STEP + (s + 5))
                v.wait_ge(up_mm, it * STEP + (s + 1))
                nc.vector.tensor_copy(xgT[s % 2], bank[s % 2][:, 0:H]).then_inc(xgT_ready, 1)
                wait(v, y_stored[s], it * 16)
                nc.vector.tensor_copy(ids_y[s], xg[s][:, H:RW]).then_inc(idy_ready, 1)

            v.sem_inc(xgT_ready, 2)
            v.sem_inc(idy_ready, STEP)

            def blocks(it):
                for s in range(STEP):
                    rows_T(it, s)

            blocks(0)
            with v.Fori(1, NBLK // STEP - 1) as it:
                blocks(it)
            for s in range(STEP):
                rows_T(NBLK // STEP - 1, s)

            v.sem_inc(summed, 4)
            with v.Fori(0, NT // 4) as it:
                chain.enter(it, 4 * (K - 1))
                for pair in range(2):
                    for k in range(K):
                        for h in (2 * pair, 2 * pair + 1):
                            if k == 0:
                                v.wait_ge(yk_loaded[h], it * 16 + 16)
                                v.wait_ge(out_stored[h], it * 16 + 16)
                            else:
                                wait_apart(v, dve, chain.base + chain.n - (1 if k < K - 1 or h % 2 == 0 else 0))
                            prev = x_sb[:, ds(it * (4 * H) + h * H, H)] if k == 0 else acc[h]
                            ins = nc.vector.scalar_tensor_tensor(acc[h], yk[h][:, k * H:(k + 1) * H],
                                                                 wts[:, ds(it * (4 * K) + (h * K + k), 1)], prev, ALU.mult, ALU.add)
                            if k < K - 1:
                                chain.n += 1
                                ins.then_inc(dve, 1)
                            else:
                                ins.then_inc(summed, 1)
                chain.leave(NT // 4)

        @block.tensor
        def _(pe):
            def mm(o, lhsT, rhs, first=True, last=True):
                return nc.tensor.matmul(o, lhsT, rhs, start=first, stop=last)

            pe.wait_ge(ld_c, 16)
            pe.wait_ge(ld_qkv, 16)
            pe.sem_inc(xn_used, 4)
            pe.sem_inc(v_mm, 1)

            def rows_to_T(b):
                for tt in range(4):
                    pe.wait_ge(xn_ready, b * 4 + (tt + 1))
                    for c in range(CH):
                        last = nc.tensor.transpose(bank[c][:, tt * P:(tt + 1) * P], xn[:, tt, c * P:(c + 1) * P], ident)
                    last.then_inc(xn_used, 1)

            def qkv(b):
                pe.wait_ge(xnT_ready, b * 2 + 4)
                cols = ((2, 0, P, None, -4), (3, P, P, q_mm, None), (4, 2 * P, 64, k_mm, 0))
                for bk_n, at, m, done, used in cols:
                    if used is not None:
                        wait(pe, rot_terms, b * 8 + used)
                    for c in range(CH):
                        last = mm(bank[bk_n][0:m, :], wqkv[:, c, at:at + m], xnT[:, c, :], c == 0, c == CH - 1)
                    if done:
                        last.then_inc(done, 1)
                pe.wait_ge(v_done, b + 1)
                for tt in range(4):
                    for c in range(CH):
                        last = mm(bank[6][:, tt * 64:(tt + 1) * 64], xnT[:, c, tt * P:(tt + 1) * P],
                                  wqkv[:, c, 320:384], c == 0, c == CH - 1)
                last.then_inc(v_mm, 1)

            rows_to_T(0)
            qkv(0)
            rows_to_T(1)
            with pe.Fori(1, NB - 1) as b:
                qkv(b)
                rows_to_T(b + 1)
            qkv(NB - 1)

            def score_q(b, g, n):
                tt, c, j = max_chunks(b)[n]
                w = QB if c < b else 128 * (tt + 1)
                before = maxes_before(b, g)
                wait(pe, sq_used, before + (n - 3))
                mm(S_Q[n % 4][:, 0:w], q_aug[:, ds(g + 4 * b, 1), tt * P:(tt + 1) * P].rearrange("p u t -> p (u t)"),
                   k_pad[:, j, ds(g * T + c * QB, w)]).then_inc(sq_ready, 1)

            def score_k(b, g, mb, st, j):
                n, before = 4 * st + j, tiles_before(b, g)
                at = 128 * max(0, st - 4 * b)
                diagonal = st >= 4 * b
                wait(pe, p_ready, before * 4 + (n - 1 if mb is not None or n < 2 else n - 3))
                o = sk_bank(mb, n)
                last = mm(o[:, at:QB], k_pad[:, j, ds(g * T + st * P, P)],
                          q_aug[:, ds(g + 4 * b, 1), at:QB].rearrange("p u t -> p (u t)"), True, not diagonal)
                if diagonal:
                    last = mm(o[:, at:at + P], ident16[:, :], kmask16[:, :], False, True)
                last.then_inc(sk_ready, 1)

            def p_times_v(b, g, st, j):
                before = tiles_before(b, g)
                at = 128 * max(0, st - 4 * b)
                pe.wait_ge(p_ready, before * 4 + (4 * st + j + 1))
                if j == 0:
                    pe.wait_ge(v_staged, before + (st + 1))
                    if st == 0:
                        wait(pe, pv_copied, g + 4 * b)
                last = mm(PV[32 * j:32 * j + 32, at:QB], v_cur[:, key_tiles(b) - 1 - st, :], p_ring[:, (4 * st + j) % 8, at:QB],
                          st == 0, False)
                if j == J - 1:
                    last.then_inc(pv_done, 1)

            def last_p_times_v(tiles, j):
                pe.wait_ge(p_ready, tiles * 4 + (j - 3))
                if j == 0:
                    pe.wait_ge(v_staged, tiles)
                last = mm(PV[32 * j:32 * j + 32, QB - P:QB], v_cur[:, 0, :], p_ring[:, 4 + j, QB - P:QB], False, True)
                if j == J - 1:
                    last.then_inc(pv_done, 1)

            def transpose_max(u):
                pe.wait_ge(split_done, u + 1)
                wait(pe, mrow_placed, u * J)
                for tt in range(4):
                    last = nc.tensor.transpose(bank16[7][:, tt * P:(tt + 1) * P], m_stage[:, tt, :], ident16[:, :])
                last.then_inc(mT_ready, 1)

            def body(b, g, mb, mg, odd):
                nst = key_tiles(b)
                beside = chunks_beside(b, mb) if mb is not None else [()] * nst
                if mb is not None:
                    pe.wait_ge(qk_placed, 32 * J * (mb + 2))
                else:
                    pe.wait_ge(sq_used, maxes_before(NB, 0))
                pe.wait_ge(mrow_placed, g * J + (4 * b + 1) * J)
                for st in range(nst):
                    if st == nst // 2 and has_next(mb, mg):
                        transpose_max(g + (4 * b + 1))
                    todo = beside[st]
                    for j in range(J):
                        score_k(b, g, mb, st, j)
                        for n in todo[len(todo) * j // J:len(todo) * (j + 1) // J]:
                            score_q(mb, mg, n)
                        if st:
                            p_times_v(b, g, st - 1, j)
                        elif not (isinstance(g, int) and b + g == 0):
                            last_p_times_v(tiles_before(b, g), j)

            pe.wait_ge(consts16, 1)
            pe.wait_ge(v_done, NB + 1)
            pe.wait_ge(qk_placed, 32 * J * 2)
            for g in range(2):
                for n in range(16):
                    score_q(0, g, n)
            transpose_max(0)
            bodies(pe, body)
            for j in range(J):
                last_p_times_v(tiles_before(NB - 1, NKV), j)

            pe.wait_ge(ld_late, 16 * 4)
            for n in range(NT):
                if n % 4 == 0:
                    pe.wait_ge(o_done, n // 4 * NKV + NKV)
                if n == 2:
                    pe.wait_ge(pv_copied, UNITS)
                wait(pe, x1_done, n - 3)
                for g in range(NKV):
                    at = (n // 4 * NKV + g) * QB + n % 4 * P
                    last = mm(C_BANKS[n % 4][:, 0:H], o_nrm[:, at:at + P], wo[:, g, :], g == 0, g == NKV - 1)
                last.then_inc(wo_mm, 1)

            def xn2_to_T(b):
                wait(pe, xn2T_ready, 2 * (b - 1))
                for n in range(4 * b, 4 * b + 4):
                    pe.wait_ge(xn2_ready, n + 1)
                    for c in range(CH):
                        last = nc.tensor.transpose(bank[2 + 2 * (b % 2) + c][:, n % 4 * P:(n % 4 + 1) * P],
                                                   xn2_all[:, n * H + c * P:n * H + (c + 1) * P], ident)
                last.then_inc(xn2_used, 1)

            xn2_to_T(0)
            for b in range(NB):
                if b + 1 < NB:
                    xn2_to_T(b + 1)
                if b == 0:
                    pe.wait_ge(x1_done, NT)
                pe.wait_ge(xn2T_ready, 2 * b + 2)
                for n in range(4 * b, 4 * b + 4):
                    for c in range(CH):
                        last = mm(bank[6 + n // 8][:, n % 8 * E:(n % 8 + 1) * E], xn2T[:, c, n * P:(n + 1) * P], gate_sb[:, c, :],
                                  c == 0, c == CH - 1)
                if b % 2:
                    last.then_inc(logit_mm, 1)

            for n in range(NT):
                pe.wait_ge(hot_ready, n // 8 + 1)
                for k in range(K):
                    last = mm(bank[n // 4][0:E, n % 4 * P:(n % 4 + 1) * P], hot_v[:, n, k, :], ident16[:, :], k == 0, k == K - 1)
                if n % 4 == 3:
                    last.then_inc(hot_mm, 1)
            pe.wait_ge(padded, 1)
            mm(bank[5][0:E, 0:1], tri_before, cnt[:, 2:3])
            mm(bank[5][0:E, 1:2], tri_upto, cnt[:, 2:3]).then_inc(base_mm, 1)
            pe.wait_ge(past_ready, 1)
            mm(bank[5][0:1, 2:2 + NBLK], ones_col, past_end).then_inc(eob_mm, 1)
            pe.wait_ge(slotT_ready, 1)
            for n in range(NT):
                last = nc.tensor.transpose(bank[6 + n // 8][:, n % 8 * E:(n % 8 + 1) * E], cum[:, n * P:(n + 1) * P], ident[0:E, 0:E])
                if n % 8 == 7:
                    last.then_inc(slotT_mm, 1)
            pe.wait_ge(eob_ready, 1)
            pe.sem_inc(shd_mm, 4)
            with pe.Fori(0, NB) as b:
                for m in range(4):
                    pe.wait_ge(hs_ready, b * 4 + (m + 1))
                    for half in range(2):
                        at = half * SI + m * HI
                        for c in range(CH):
                            last = mm(bank[2 * half + m % 2][0:HI, :], sh1[:, c, at:at + HI], xn2T[:, c, ds(b * QB, QB)],
                                      c == 0, c == CH - 1)
                    last.then_inc(sh_mm, 1)
                pe.wait_ge(hs_ready, b * 4 + 6)
                for tt in range(4):
                    pe.wait_ge(sh_added, b * 4 + (tt + 1))
                    for m in range(4):
                        last = mm(bank[4 + tt % 2][:, 0:H], hs[:, m, tt * P:(tt + 1) * P], sh2[:, m, :], m == 0, m == 3)
                    last.then_inc(shd_mm, 1)

            def rows_T(it, s):
                pe.wait_ge(xg_loaded[s], it * 16 + 16)
                pe.wait_ge(xgT_ready, it * STEP + (s + 1))
                for c in range(CH):
                    last = nc.tensor.transpose(bank[s % 2][:, c * P:(c + 1) * P], xg[s][:, c * P:(c + 1) * P], ident)
                last.then_inc(xg_T, 1)

            def up(it, s):
                pe.wait_ge(w_loaded[s % 4], it * (STEP // 4 * 32) + (s // 4 * 32 + 32))
                pe.wait_ge(xgT_ready, it * STEP + (s + 3))
                pe.wait_ge(h_ready, it * STEP + (s + 1))
                for i in range(2):
                    for c in range(CH):
                        last = mm(bank[2 + s % 2][0:HI, i * P:(i + 1) * P], w1s[s % 4][:, c, i * HI:(i + 1) * HI],
                                  xgT[s % 2][:, c * P:(c + 1) * P], c == 0, c == CH - 1)
                last.then_inc(up_mm, 1)

            def down(it, s):
                pe.wait_ge(h_ready, it * STEP + (s + 3))
                pe.wait_ge(y_ready, it * STEP + (s + 1))
                for i in range(2):
                    last = mm(bank[4 + s % 2][:, 0:H], hT[s % 2][:, i * P:(i + 1) * P], w2s[s % 4][:, i, :], i == 0, i == 1)
                last.then_inc(down_mm, 1)

            pe.wait_ge(sh_added, NT + 2)
            pe.sem_inc(xg_T, 4)
            pe.sem_inc(up_mm, 2)
            pe.sem_inc(down_mm, 4)
            rows_T(0, 0)
            rows_T(0, 1)
            up(0, 0)
            with pe.Fori(0, NBLK // STEP - 1) as it:
                for s in range(STEP):
                    rows_T(it + (s + 2) // STEP, (s + 2) % STEP)
                    up(it + (s + 1) // STEP, (s + 1) % STEP)
                    down(it, s)
            end = NBLK // STEP - 1
            for s in range(STEP):
                if s < STEP - 2:
                    rows_T(end, s + 2)
                if s < STEP - 1:
                    up(end, s + 1)
                down(end, s)


_INS = ["x", "w_qkv", "b_q", "b_k", "b_v", "b_o", "w_o", "gate", "w_sh1", "w_sh2", "w1", "w2", "trig", "cst"]


def constants():
    freqs = (np.float32(10000.0) ** -(np.arange(0, H, 2, dtype=np.float32) / np.float32(H)))[:HD // 2]
    ang = np.outer(freqs, np.arange(T, dtype=np.float32)).astype(np.float32)
    rows = np.tile(ang.astype(np.float64), (P // (HD // 2), 1))
    trig = np.concatenate([np.cos(rows), np.sin(rows)], axis=1).astype(np.float32)
    p, c = np.arange(P)[:, None], np.arange(512)[None, :]
    cst = np.zeros((P, 1121), np.float32)
    cst[:, 0:128] = np.eye(P)
    cst[:, 128:640] = np.where(c <= 384 + p, 0.0, BIG)
    cst[:, 640:768] = np.where(c[:, :P] >= p, 0.0, BIG)
    cst[:, 768:832] = np.arange(E)
    cst[:, 832:896] = p < c[:, :E]
    cst[:, 896:960] = p <= c[:, :E]
    cst[:, 960:1120] = np.arange(NBLK) * P
    cst[:, 1120] = 1.0
    return trig, cst


def laid_out(a):
    def chunks(w, rows):
        return w.reshape(-1, rows, w.shape[-1]).transpose(1, 0, 2)

    def q_cols(w):
        w = w.reshape(-1, NKV, J, HD // 2, 2).transpose(0, 2, 1, 3, 4)
        return [w[..., n].reshape(w.shape[0], -1) for n in range(2)]

    def k_cols(w):
        w = w.reshape(-1, NKV, HD // 2, 2)
        return [w[..., n].reshape(w.shape[0], -1) for n in range(2)]

    qe, qo = q_cols(a["L0_attn_Wq"])
    ke, ko = k_cols(a["L0_attn_Wk"])
    bqe, bqo = q_cols(a["L0_attn_bq"][None, :])
    bke, bko = k_cols(a["L0_attn_bk"][None, :])
    wo = np.zeros((J, 32, NKV, H), np.float32)
    wo[:, :HD] = a["L0_attn_Wo"].reshape(NKV, J, HD, H).transpose(1, 2, 0, 3)
    trig, cst = constants()
    return {
        "x": a["L0_attn_x"],
        "w_qkv": chunks(np.concatenate([qe, qo, ke, ko, a["L0_attn_Wv"]], axis=1), P),
        "b_q": np.stack([bqe[0], bqo[0]], axis=1),
        "b_k": np.concatenate([bke[0], bko[0]])[:, None],
        "b_v": np.broadcast_to(a["L0_attn_bv"], (P, NKV * HD)),
        "b_o": np.broadcast_to(a["L0_attn_bo"], (P, H)),
        "w_o": wo.reshape(P, NKV, H),
        "gate": chunks(a["L0_ffn_gate_w"].T, P),
        "w_sh1": chunks(a["L0_ffn_shared_gate_up"].T, P),
        "w_sh2": chunks(a["L0_ffn_shared_down"].T, HI),
        "w1": a["L0_ffn_experts_w1"].reshape(E, I, CH, P).transpose(3, 0, 2, 1),
        "w2": a["L0_ffn_experts_w2"].reshape(E, H, 2, HI).transpose(3, 0, 2, 1),
        "trig": trig,
        "cst": cst,
    }


def kernel(**inputs):
    import concourse.bacc as _bacc
    from concourse.bass_utils import run_bass_kernel_spmd as _run

    arrays = {f"in_{k}": np.ascontiguousarray(v) for k, v in laid_out({k: np.asarray(v) for k, v in inputs.items()}).items()}
    nc = _bacc.Bacc("TRN2", target_bir_lowering=False, num_devices=1)
    args = [nc.dram_tensor(f"in_{n}", arrays[f"in_{n}"].shape, mybir.dt.from_np(arrays[f"in_{n}"].dtype),
                           kind="ExternalInput").ap() for n in _INS]
    out = nc.dram_tensor("out", (1, T, H), mybir.dt.float32, kind="ExternalOutput").ap()
    preln_attention_moe(nc, *args, out)
    r = _run(nc, [arrays], core_ids=[0])
    return r.results[0]["out"]
```
